# Optimizing a Trainium2 kernel written in Bass

```python
import numpy as np
import jax
import jax.numpy as jnp

def _softmax(x, axis=-1):
    return jax.nn.softmax(x, axis=axis)

def _gelu(x):
    return jax.nn.gelu(x, approximate=True)

def _silu(x):
    return jax.nn.silu(x)

def _sigmoid(x):
    return jax.nn.sigmoid(x)

def _layernorm(x, axis=-1, eps=1e-05):
    m = jnp.mean(x, axis=axis, keepdims=True)
    v = jnp.var(x, axis=axis, keepdims=True)
    return (x - m) / jnp.sqrt(v + eps)

def _scatter_add(tgt, idx, src, axis=0):
    return tgt.at[idx].add(src)

def _segment_sum(src, seg, n):
    return jax.ops.segment_sum(src, seg, n)
kernel_name = 'mk_flamingo_gated_d1_seqx_r8_c6b47f'

def setup_inputs(seed: int=0):
    np.random.seed(seed)
    _w = jnp.asarray

    def _rec_inputs():
        import jax
        import jax.numpy as jnp
        _rk = jax.random.key(seed)
        x = 4.136e-05 + 0.9999 * jax.random.normal(jax.random.fold_in(_rk, 1), (4, 256, 256), jnp.float32)
        _lenS = 256 - jax.random.randint(jax.random.fold_in(_rk, 7), (4,), 0, max(1, 256 // 4) + 1, jnp.int32)
        _lenS2 = 256 - jax.random.randint(jax.random.fold_in(_rk, 8), (4,), 0, max(1, 256 // 4) + 1, jnp.int32)
        _ctx_1024P = jax.random.normal(jax.random.fold_in(_rk, 11), (4, 16, 128), jnp.float32)
        _ctx_1024c = jax.random.dirichlet(jax.random.fold_in(_rk, 511), 0.3 * jnp.ones((16,), jnp.float32), (4, 256))
        _ctx_1024t = jnp.einsum('bsk,bkd->bsd', _ctx_1024c, _ctx_1024P)
        _ctx_1024t = _ctx_1024t * jax.lax.rsqrt(jnp.mean(jnp.square(_ctx_1024t)) + 1e-12) * 0.953939
        ctx_1024 = -0.000292821 + 1.00034 * (_ctx_1024t + 0.3 * jax.random.normal(jax.random.fold_in(_rk, 611), (4, 256, 128), jnp.float32))
        _g = jax.random.normal(jax.random.fold_in(_rk, 9001), (2, 1), jnp.float32)
        _g = jnp.sign(_g) * jnp.maximum(jnp.abs(_g), 1.0) + (_g == 0) * 1.0
        g_xattn = _g[0]
        g_ffn = _g[1]
        return (x, ctx_1024, g_xattn, g_ffn)
    x, ctx_1024, g_xattn, g_ffn = _rec_inputs()

    def _L0_xattn_setup():
        import jax, jax.numpy as jnp
        import numpy as np
        import math
        B, L, DM = (2, 256, 128)
        DS, DC, EXP = (16, 4, 2)
        DI = EXP * DM
        DR = math.ceil(DM / 16)
        DT_MIN, DT_MAX, DT_FLOOR = (0.001, 0.1, 0.0001)

        def _ssm_forward(hidden_states, z, in_proj_w, conv_w, conv_b, x_proj_w, dt_proj_w, dt_proj_b, A_log, D):
            b = hidden_states.shape[0]
            x = jnp.einsum('ed,bld->bel', in_proj_w, hidden_states)
            xp = jnp.pad(x, ((0, 0), (0, 0), (DC - 1, 0)))
            xc = jax.lax.conv_general_dilated(xp, conv_w[:, None, :], window_strides=(1,), padding='VALID', dimension_numbers=('NCH', 'OIH', 'NCH'), feature_group_count=DI)
            u = jax.nn.silu(xc + conv_b[None, :, None])
            x_dbl = jnp.einsum('ke,bel->bkl', x_proj_w, u)
            dt_lo = x_dbl[:, :DR]
            Bm = x_dbl[:, DR:DR + DS]
            Cm = x_dbl[:, DR + DS:]
            delta = jax.nn.softplus(jnp.einsum('er,brl->bel', dt_proj_w, dt_lo) + dt_proj_b[None, :, None])
            A = -jnp.exp(A_log)

            def step(state, xs):
                d_t, B_t, C_t, u_t = xs
                dA = jnp.exp(d_t[..., None] * A)
                state = state * dA + (d_t * u_t)[..., None] * B_t[:, None, :]
                y_t = jnp.einsum('ben,bn->be', state, C_t)
                return (state, y_t)
            xs = (jnp.moveaxis(delta, -1, 0), jnp.moveaxis(Bm, -1, 0), jnp.moveaxis(Cm, -1, 0), jnp.moveaxis(u, -1, 0))
            state0 = jnp.zeros((b, DI, DS), delta.dtype)
            _, ys = jax.lax.scan(step, state0, xs)
            y = jnp.moveaxis(ys, 0, -1)
            y = y + D[None, :, None] * u
            y = y * jax.nn.silu(z)
            return jnp.swapaxes(y, 1, 2)
        key = jax.random.key(seed)
        ks = jax.random.split(key, 8)
        hidden_states = jax.random.normal(ks[0], (B, L, DM), jnp.float32)
        z = jax.random.normal(ks[1], (B, DI, L), jnp.float32)
        in_proj_w = jax.random.normal(ks[2], (DI, DM), jnp.float32) * DM ** (-0.5)
        conv_w = jax.random.normal(ks[3], (DI, DC), jnp.float32) * DC ** (-0.5)
        conv_b = jnp.zeros((DI,), jnp.float32)
        x_proj_w = jax.random.normal(ks[4], (DR + 2 * DS, DI), jnp.float32) * DI ** (-0.5)
        dt_std = DR ** (-0.5)
        dt_proj_w = jax.random.uniform(ks[5], (DI, DR), jnp.float32, -dt_std, dt_std)
        dt = jnp.exp(jax.random.uniform(ks[6], (DI,), jnp.float32) * (math.log(DT_MAX) - math.log(DT_MIN)) + math.log(DT_MIN))
        dt = jnp.clip(dt, DT_FLOOR)
        dt_proj_b = dt + jnp.log(-jnp.expm1(-dt))
        A_log = jnp.log(jnp.broadcast_to(jnp.arange(1, DS + 1, dtype=jnp.float32), (DI, DS)))
        D = jnp.ones((DI,), jnp.float32)
        return dict(hidden_states=hidden_states, z=z, in_proj_w=in_proj_w, conv_w=conv_w, conv_b=conv_b, x_proj_w=x_proj_w, dt_proj_w=dt_proj_w, dt_proj_b=dt_proj_b, A_log=A_log, D=D)
    _L0_xattn_all = _L0_xattn_setup()
    _L0_xattn_in = {k: v for k, v in _L0_xattn_all.items() if k in ('in_proj_w', 'conv_w', 'conv_b', 'x_proj_w', 'dt_proj_w', 'dt_proj_b', 'A_log', 'D')}
    del _L0_xattn_all

    def _L0_ffn_setup():
        import jax, jax.numpy as jnp
        import numpy as np
        EPS = 1e-08

        def _quantize(w):
            gamma = jnp.mean(jnp.abs(w))
            return jnp.clip(jnp.round(w / (gamma + EPS)), -1.0, 1.0)

        def _bitlinear(x, w):
            return jnp.matmul(x, _quantize(w).T)
        key = jax.random.key(seed)
        k1, k2, k3, k4 = jax.random.split(key, 4)
        d, h = (256, 704)
        x = jax.random.normal(k1, (4, 256, d), dtype=jnp.float32)
        w1 = jax.random.normal(k2, (h, d), dtype=jnp.float32)
        w2 = jax.random.normal(k3, (h, d), dtype=jnp.float32)
        w3 = jax.random.normal(k4, (d, h), dtype=jnp.float32)
        return {'x': x, 'w1': w1, 'w2': w2, 'w3': w3}
    _L0_ffn_all = _L0_ffn_setup()
    _L0_ffn_in = {k: v for k, v in _L0_ffn_all.items() if k in ('w1', 'w2', 'w3')}
    del _L0_ffn_all
    return {'x': x, 'ctx_1024': ctx_1024, 'g_xattn': g_xattn, 'g_ffn': g_ffn, 'L0_xattn_in_proj_w': _L0_xattn_in['in_proj_w'], 'L0_xattn_conv_w': _L0_xattn_in['conv_w'], 'L0_xattn_conv_b': _L0_xattn_in['conv_b'], 'L0_xattn_x_proj_w': _L0_xattn_in['x_proj_w'], 'L0_xattn_dt_proj_w': _L0_xattn_in['dt_proj_w'], 'L0_xattn_dt_proj_b': _L0_xattn_in['dt_proj_b'], 'L0_xattn_A_log': _L0_xattn_in['A_log'], 'L0_xattn_D': _L0_xattn_in['D'], 'L0_ffn_w1': _L0_ffn_in['w1'], 'L0_ffn_w2': _L0_ffn_in['w2'], 'L0_ffn_w3': _L0_ffn_in['w3']}

def reference(x, ctx_1024, g_xattn, g_ffn, L0_xattn_in_proj_w, L0_xattn_conv_w, L0_xattn_conv_b, L0_xattn_x_proj_w, L0_xattn_dt_proj_w, L0_xattn_dt_proj_b, L0_xattn_A_log, L0_xattn_D, L0_ffn_w1, L0_ffn_w2, L0_ffn_w3):
    import jax
    import jax.numpy as jnp

    def _L0_xattn_ref(hidden_states, z, in_proj_w, conv_w, conv_b, x_proj_w, dt_proj_w, dt_proj_b, A_log, D):
        import jax, jax.numpy as jnp
        import numpy as np
        import math
        B, L, DM = (2, 256, 128)
        DS, DC, EXP = (16, 4, 2)
        DI = EXP * DM
        DR = math.ceil(DM / 16)
        DT_MIN, DT_MAX, DT_FLOOR = (0.001, 0.1, 0.0001)

        def _ssm_forward(hidden_states, z, in_proj_w, conv_w, conv_b, x_proj_w, dt_proj_w, dt_proj_b, A_log, D):
            b = hidden_states.shape[0]
            x = jnp.einsum('ed,bld->bel', in_proj_w, hidden_states)
            xp = jnp.pad(x, ((0, 0), (0, 0), (DC - 1, 0)))
            xc = jax.lax.conv_general_dilated(xp, conv_w[:, None, :], window_strides=(1,), padding='VALID', dimension_numbers=('NCH', 'OIH', 'NCH'), feature_group_count=DI)
            u = jax.nn.silu(xc + conv_b[None, :, None])
            x_dbl = jnp.einsum('ke,bel->bkl', x_proj_w, u)
            dt_lo = x_dbl[:, :DR]
            Bm = x_dbl[:, DR:DR + DS]
            Cm = x_dbl[:, DR + DS:]
            delta = jax.nn.softplus(jnp.einsum('er,brl->bel', dt_proj_w, dt_lo) + dt_proj_b[None, :, None])
            A = -jnp.exp(A_log)

            def step(state, xs):
                d_t, B_t, C_t, u_t = xs
                dA = jnp.exp(d_t[..., None] * A)
                state = state * dA + (d_t * u_t)[..., None] * B_t[:, None, :]
                y_t = jnp.einsum('ben,bn->be', state, C_t)
                return (state, y_t)
            xs = (jnp.moveaxis(delta, -1, 0), jnp.moveaxis(Bm, -1, 0), jnp.moveaxis(Cm, -1, 0), jnp.moveaxis(u, -1, 0))
            state0 = jnp.zeros((b, DI, DS), delta.dtype)
            _, ys = jax.lax.scan(step, state0, xs)
            y = jnp.moveaxis(ys, 0, -1)
            y = y + D[None, :, None] * u
            y = y * jax.nn.silu(z)
            return jnp.swapaxes(y, 1, 2)
        return _ssm_forward(hidden_states, z, in_proj_w, conv_w, conv_b, x_proj_w, dt_proj_w, dt_proj_b, A_log, D)

    def _L0_ffn_ref(x, w1, w2, w3):
        import jax, jax.numpy as jnp
        import numpy as np
        EPS = 1e-08

        def _quantize(w):
            gamma = jnp.mean(jnp.abs(w))
            return jnp.clip(jnp.round(w / (gamma + EPS)), -1.0, 1.0)

        def _bitlinear(x, w):
            return jnp.matmul(x, _quantize(w).T)
        x1 = _bitlinear(x, w1)
        x2 = _bitlinear(x, w2)
        hidden = jax.nn.sigmoid(x1) * x2
        return _bitlinear(hidden, w3)
    x = x + jnp.tanh(g_xattn[0]) * _L0_xattn_ref(ctx_1024, _layernorm(x, axis=-1), L0_xattn_in_proj_w, L0_xattn_conv_w, L0_xattn_conv_b, L0_xattn_x_proj_w, L0_xattn_dt_proj_w, L0_xattn_dt_proj_b, L0_xattn_A_log, L0_xattn_D)
    x = x + jnp.tanh(g_ffn[0]) * _L0_ffn_ref(_layernorm(x, axis=-1), L0_ffn_w1, L0_ffn_w2, L0_ffn_w3)
    return x

_drawn_inputs = setup_inputs


def setup_inputs(seed=0):
    import zlib

    import numpy as np

    out = dict(_drawn_inputs(seed))
    spreads = {'L0_xattn_conv_b': (0.0, 0.1), 'L0_xattn_D': (1.0, 0.2)}
    factors = {'L0_xattn_dt_proj_w': 4.781}
    for name, (base, spread) in spreads.items():
        noise = np.random.default_rng([zlib.crc32(name.encode()), seed]).standard_normal(out[name].shape)
        drawn = base * np.exp(spread * noise) if base else spread * noise
        out[name] = jnp.asarray(drawn.astype(out[name].dtype))
    for name, factor in factors.items():
        out[name] = (out[name] * factor).astype(out[name].dtype)
    return out
```

```python
from contextlib import ExitStack

import concourse.bass as bass
from concourse import mybir

F32 = mybir.dt.float32
BF16 = mybir.dt.bfloat16
ALU = mybir.AluOpType
ACT = mybir.ActivationFunctionType
AX_X = mybir.AxisListType.X

P = 128
NB = 4
L = 256
DM = 128
DI = 256
EH = DI // P
DS = 16
DR = 8
DC = 4
H = 704
HC = 6
HF = H // P
HL = H - HF * P
KD = L // P
NG = 4
NGRP = DS // NG
TPB = NGRP * EH
NT = NB * TPB
QW = 512
LN_EPS = 1e-5
Q_EPS = 1e-8

N_DECAY = 3
N_STATE = 3
N_PROD = 3
N_CREP = 2
LAG = 2

C_CONVW, C_CONVB, C_DTB, C_ALOG, C_D = 0, DC, DC + 1, DC + 2, DC + 2 + DS
NPAR = C_D + 1
BC = 2 * DS
DT0 = 3 * BC


def fill_slots():
    slots = [[] for _ in range(NT + 14)]
    slots[0] += [("conv", 1, 0)]
    slots[1] += [("xdbl", 1, 0), ("conv", 2, 0)]
    slots[2] += [("xdbl", 2, 0), ("conv", 3, 0)]
    slots[3] += [("xdbl", 3, 0)]
    slots[4] += [("delta", 1, 0), ("norm", 0, 0)]
    slots[5] += [("gate", 0, 0), ("quant", 0, 0)]
    slots[6] += [("quant", 1, 0), ("gate", 1, 0)]
    slots[7] += [("quant", 2, 0)]
    slots[8] += [("gate", 2, 0)]
    slots[9] += [("gate", 3, 0)]
    for b in range(NB):
        at = TPB * (b + 1)
        slots[at + 2] += [("comb", b, 0)]
        slots[at + 3] += [("resid", b, 0)]
        slots[at + 4] += [("split", b, 0)]
        for h in range(HC):
            slots[at + 5 + h] += [("up", b, h)]
            slots[at + 6 + h] += [("down", b, h)]
        slots[at + 5 + HC] += [("out", b, 0)]
    return slots


def gated_ssm_ffn_kernel(nc, x, ctxT, gains, winT, par, xwT, dtwT, w1T, w2T, w3T, out):
    slots = fill_slots()
    with ExitStack() as es:
        def sb(name, shape, dt=F32):
            return es.enter_context(nc.sbuf_tensor(name, shape, dt))

        def psum(name, cols):
            return es.enter_context(nc.psum_tensor(name, [P, cols], F32))

        def sem(name):
            return es.enter_context(nc.semaphore(name))

        par_sb = sb("par_sb", [P, EH, NPAR])
        half_conv = sb("half_conv", [P, EH, DC + 1])
        a_neg = sb("a_neg", [P, EH, DS])
        a_exp = sb("a_exp", [P, EH, DS])
        gains_sb = sb("gains_sb", [P, 2])
        tanh_g = sb("tanh_g", [P, 2])
        half_tanh_g = sb("half_tanh_g", [P, 2])
        win_sb = sb("win_sb", [P, DI])
        ctx_sb = sb("ctx_sb", [P, NB, L])
        xw_in = sb("xw_in", [P, EH, BC + DR])
        xw_sb = sb("xw_sb", [P, EH, DT0 + DR])
        dtw_sb = sb("dtw_sb", [P, DI])
        x_sb = sb("x_sb", [P, NB, KD, L])
        w_up_in = sb("w_up_in", [P, 2, KD, H])
        w_down_in = sb("w_down_in", [P, HC, L])
        w_below = sb("w_below", [P, HC * L], BF16)
        w_up_q = sb("w_up_q", [P, KD, 2 * H], BF16)
        w_down_q = sb("w_down_q", [P, HC, L])
        abs_sum = sb("abs_sum", [P, 4])
        thr = sb("thr", [P, 4])
        thr_neg = sb("thr_neg", [P, 4])
        ident = sb("ident", [P, P])
        ones = sb("ones", [P, P])
        row_of3 = sb("row_of3", [3 * BC, BC], BF16)
        pick = sb("pick", [3 * BC, BC, P], BF16)

        conv = sb("conv", [P, NB, EH, L])
        conv_t = sb("conv_t", [P, NB, EH, L])
        u_sb = sb("u_sb", [P, NB, EH, L])
        dt_low = sb("dt_low", [P, NB, L])
        bc_parts = sb("bc_parts", [3 * BC, NB, L], BF16)
        bc_rest = sb("bc_rest", [3 * BC, NB, L])
        bc_mid = sb("bc_mid", [3 * BC, NB, L], BF16)
        dt_x = sb("dt_x", [P, NB, EH, L])
        dt_abs = sb("dt_abs", [P, NB, EH, L])
        dt_ln = sb("dt_ln", [P, NB, EH, L])
        delta = sb("delta", [P, NB, EH, L])
        du = sb("du", [P, NB, EH, L])

        decay = [sb(f"decay{i}", [P, NG, L]) for i in range(N_DECAY)]
        state = [sb(f"state{i}", [P, NG, L]) for i in range(N_STATE)]
        prod = [sb(f"prod{i}", [P, NG, L]) for i in range(N_PROD)]
        c_rep = [sb(f"c_rep{i}", [P, NG, L]) for i in range(N_CREP)]

        ln_stats = sb("ln_stats", [P, NB * KD, 6])
        ln_mv = sb("ln_mv", [P, NB * KD, 2])
        ln_ve = sb("ln_ve", [P, NB * KD])
        ln_half = sb("ln_half", [P, NB * KD])
        ln_rstd = sb("ln_rstd", [P, NB * KD])
        minus_half = sb("minus_half", [P, NB * KD])
        z_half, z_tanh, gate = dt_x, conv_t, dt_ln

        y_d = sb("y_d", [P, EH, L])
        mixed = sb("mixed", [P, EH, L])
        x1_sb = sb("x1_sb", [P, 2, KD, L])
        st2 = sb("st2", [P, NB * KD, 6])
        mv2 = sb("mv2", [P, NB * KD, 2])
        ve2 = sb("ve2", [P, NB * KD])
        rstd2 = sb("rstd2", [P, NB * KD])
        shift2 = sb("shift2", [P, NB * KD])
        z2_sb = sb("z2_sb", [P, KD, L])
        z2_hi = sb("z2_hi", [P, KD, L], BF16)
        z2_rest = sb("z2_rest", [P, KD, L])
        z2_mid = sb("z2_mid", [P, KD, L], BF16)
        z2_lo = sb("z2_lo", [P, KD, L], BF16)
        up_tanh = sb("up_tanh", [P, 2, L])
        hidden = sb("hidden", [P, 2, HC, L])

        ps_b = psum("ps_b", 2 * QW)
        ps_db = psum("ps_db", 2 * QW)
        ps_c = psum("ps_c", QW)
        ps_y = psum("ps_y", QW)
        ps_w0 = psum("ps_w0", QW)
        ps_w1 = psum("ps_w1", QW)

        ld_par, ld_win, ld_ctx0, ld_ctx, ld_xw, ld_dtw = (sem(n) for n in (
            "ld_par", "ld_win", "ld_ctx0", "ld_ctx", "ld_xw", "ld_dtw"))
        ld_g, ld_x, ld_w1, ld_w2, ld_w3, ld_w3l = (sem(n) for n in (
            "ld_g", "ld_x", "ld_w1", "ld_w2", "ld_w3", "ld_w3l"))
        ident_ready, rows_ready, const_ready = sem("ident_ready"), sem("rows_ready"), sem("const_ready")
        pool_init = sem("pool_init")
        pick_ready = sem("pick_ready")
        half_conv_ready, a_exp_ready, a_ready = sem("half_conv_ready"), sem("a_exp_ready"), sem("a_ready")
        xw_ready, decay_zeroed = sem("xw_ready"), sem("decay_zeroed")
        tanh_g_ready, half_g_ready = sem("tanh_g_ready"), sem("half_g_ready")
        in_done, tap_done, conv_step = sem("in_done"), sem("tap_done"), sem("conv_step")
        conv_tanh_done, u_done = sem("conv_tanh_done"), sem("u_done")
        rows_done, dt_low_done, bc_hi_done = sem("rows_done"), sem("dt_low_done"), sem("bc_hi_done")
        bc_rest_done, bc_mid_done, bc_lo_done = sem("bc_rest_done"), sem("bc_mid_done"), sem("bc_lo_done")
        dt_done, dt_x_done, dt_abs_done = sem("dt_done"), sem("dt_x_done"), sem("dt_abs_done")
        dt_exp_done, dt_ln_done = sem("dt_exp_done"), sem("dt_ln_done")
        delta_done, du_done = sem("delta_done"), sem("du_done")
        b_rep_done, c_psum_done, c_rep_done = sem("b_rep_done"), sem("c_psum_done"), sem("c_rep_done")
        decay_done, db_done, scan_done = sem("decay_done"), sem("db_done"), sem("scan_done")
        prod_done, sum_done = sem("prod_done"), sem("sum_done")
        abs_zeroed, abs_done, gamma_done = sem("abs_zeroed"), sem("abs_done"), sem("gamma_done")
        thr_step, below_done, quant_done = sem("thr_step"), sem("below_done"), sem("quant_done")
        stats_done, mv_done, ve_done = sem("stats_done"), sem("mv_done"), sem("ve_done")
        rstd_done, ln_half_done = sem("rstd_done"), sem("ln_half_done")
        z_half_done, z_tanh_done, gate_done = sem("z_half_done"), sem("z_tanh_done"), sem("gate_done")
        y_d_done, mixed_done, mixed_t_done = sem("y_d_done"), sem("mixed_done"), sem("mixed_t_done")
        x1_done, st2_done, mv2_done = sem("x1_done"), sem("st2_done"), sem("mv2_done")
        ve2_done, rstd2_done, shift2_done = sem("ve2_done"), sem("rstd2_done"), sem("shift2_done")
        z2_done, z2_t_done, hi_done = sem("z2_done"), sem("z2_t_done"), sem("hi_done")
        rest_done, mid_done, lo_done = sem("rest_done"), sem("mid_done"), sem("lo_done")
        up_done, up_tanh_done, hidden_done = sem("up_done"), sem("up_tanh_done"), sem("hidden_done")
        down_done, out_done, stored = sem("down_done"), sem("out_done"), sem("stored")

        def unit_end(b):
            return 1 if b == 0 else 2

        UNITS = {0: slice(0, 1), 1: slice(1, NB)}

        def up_bank(b, h):
            return ps_c if b == NB - 1 and h % 2 else ps_w0

        block = es.enter_context(nc.Block())

        @block.sync
        def _(sp):
            sp.dma_start(ctx_sb[:, 0, :], ctxT[:, 0, :]).then_inc(ld_ctx0, 16)
            sp.dma_start(win_sb[:], winT).then_inc(ld_win, 16)
            sp.dma_start(par_sb[:], par.rearrange("(h p) c -> p h c", p=P)).then_inc(ld_par, 16)
            sp.dma_start(xw_in[:], xwT.rearrange("(h p) c -> p h c", p=P)).then_inc(ld_xw, 16)
            sp.dma_start(dtw_sb[DT0:DT0 + DR, :], dtwT).then_inc(ld_dtw, 16)
            sp.dma_start(ctx_sb[:, 1:NB, :], ctxT[:, 1:NB, :]).then_inc(ld_ctx, 16)
            sp.dma_start(gains_sb[:], gains.partition_broadcast(P)).then_inc(ld_g, 16)
            sp.dma_start(x_sb[:], x.rearrange("b (t p) d -> p b t d", p=P)).then_inc(ld_x, 16)
            sp.dma_start(w_up_in[:, 0], w1T.rearrange("(k p) h -> p k h", p=P)).then_inc(ld_w1, 16)
            sp.dma_start(w_up_in[:, 1], w2T.rearrange("(k p) h -> p k h", p=P)).then_inc(ld_w2, 16)
            sp.dma_start(w_down_in[:, 0:HF, :],
                         w3T[0:HF * P, :].rearrange("(c p) d -> p c d", p=P)).then_inc(ld_w3, 16)
            sp.dma_start(w_down_in[0:HL, HF, :], w3T[HF * P:H, :]).then_inc(ld_w3l, 16)
            for b in range(NB):
                for t in range(KD):
                    sp.wait_ge(out_done, KD * b + t + 1)
                    sp.dma_start(out[b, t * P:(t + 1) * P, :], x_sb[:, b, t, :]).then_inc(stored, 16)
            sp.wait_ge(stored, 16 * NB * KD)

        @block.gpsimd
        def _(pool):
            nc.gpsimd.memset(ident[:], 0.0).then_inc(pool_init, 1)
            nc.gpsimd.memset(row_of3[:], 0.0).then_inc(pool_init, 1)
            pool.wait_ge(pool_init, 2)
            nc.gpsimd.affine_select(out=row_of3[:], in_=row_of3[:], compare_op=ALU.not_equal, fill=1.0,
                                    base=0, pattern=[[-1, BC]], channel_multiplier=1).then_inc(pool_init, 1)
            for k in range(1, 3):
                pool.wait_ge(pool_init, 2 + k)
                nc.gpsimd.affine_select(out=row_of3[:], in_=row_of3[:], compare_op=ALU.not_equal, fill=1.0,
                                        base=-BC * k, pattern=[[-1, BC]],
                                        channel_multiplier=1).then_inc(rows_ready if k == 2 else pool_init, 1)
            nc.gpsimd.affine_select(out=ident[:], in_=ident[:], compare_op=ALU.not_equal, fill=1.0,
                                    base=0, pattern=[[-1, P]], channel_multiplier=1).then_inc(ident_ready, 1)
            nc.gpsimd.memset(ones[:], 1.0).then_inc(const_ready, 1)
            nc.gpsimd.memset(minus_half[:], -0.5).then_inc(const_ready, 1)
            nc.gpsimd.memset(abs_sum[:, 3:4], 0.0).then_inc(abs_zeroed, 1)

            def delta_u(unit):
                bs = UNITS[unit]
                pool.wait_ge(delta_done, unit + 1)
                pool.wait_ge(u_done, bs.stop)
                nc.gpsimd.tensor_tensor(du[:, bs], delta[:, bs], u_sb[:, bs], ALU.mult).then_inc(du_done, 1)

            def product(t):
                pool.wait_ge(scan_done, 2 * (t + 1))
                pool.wait_ge(c_rep_done, 2 * (t // EH + 1))
                if t >= N_PROD:
                    pool.wait_ge(sum_done, t - N_PROD + 1)
                nc.gpsimd.tensor_tensor(prod[t % N_PROD][:], state[t % N_STATE][:],
                                        c_rep[(t // EH) % N_CREP][:], ALU.mult).then_inc(prod_done, 1)

            delta_u(0)
            for s, steps in enumerate(slots):
                if s < NT:
                    product(s)
                for what, b, h in steps:
                    if what == "delta":
                        delta_u(1)
                    elif what == "norm":
                        pool.wait_ge(ve_done, 1)
                        pool.wait_ge(const_ready, 2)
                        nc.gpsimd.tensor_tensor(ln_rstd[:], ln_ve[:], minus_half[:],
                                                ALU.pow).then_inc(rstd_done, 1)
                    elif what == "resid":
                        c = slice(KD * b, KD * b + KD)
                        pool.wait_ge(ve2_done, b + 1)
                        nc.gpsimd.tensor_tensor(rstd2[:, c], ve2[:, c], minus_half[:, c],
                                                ALU.pow).then_inc(rstd2_done, 1)
                    elif what == "split":
                        pool.wait_ge(mid_done, b + 1)
                        if b > 0:
                            pool.wait_ge(up_done, HC * b)
                        nc.gpsimd.tensor_tensor(z2_lo[:], z2_rest[:], z2_mid[:],
                                                ALU.subtract).then_inc(lo_done, 1)

        @block.scalar
        def _(act):
            def conv_tap(b):
                act.wait_ge(in_done, b + 1)
                act.wait_ge(half_conv_ready, 1)
                for e in range(EH):
                    nc.scalar.activation(conv[:, b, e, :], ps_w0[:, e * L:(e + 1) * L], ACT.Identity,
                                         bias=half_conv[:, e, DC:DC + 1],
                                         scale=half_conv[:, e, DC - 1:DC]).then_inc(tap_done, 1)

            def conv_tanh(b):
                act.wait_ge(conv_step, EH * (DC - 1) * (b + 1))
                nc.scalar.activation(conv_t[:, b], conv[:, b], ACT.Tanh).then_inc(conv_tanh_done, 1)

            def split_rows(b):
                act.wait_ge(rows_done, b + 1)
                nc.scalar.activation(dt_low[DT0:DT0 + DR, b, :], ps_w1[DT0:DT0 + DR, 0:L],
                                     ACT.Copy).then_inc(dt_low_done, 1)
                nc.scalar.activation(bc_parts[:, b, :], ps_w1[0:3 * BC, 0:L],
                                     ACT.Copy).then_inc(bc_hi_done, 1)

            def step_size(b):
                act.wait_ge(dt_done, b + 1)
                for e in range(EH):
                    nc.scalar.activation(dt_x[:, b, e, :], ps_w0[:, e * L:(e + 1) * L], ACT.Identity,
                                         bias=par_sb[:, e, C_DTB:C_DTB + 1]).then_inc(dt_x_done, 1)
                act.wait_ge(dt_x_done, EH * (b + 1))
                nc.scalar.activation(dt_abs[:, b], dt_x[:, b], ACT.Abs).then_inc(dt_abs_done, 1)

            def middle_rows(b):
                act.wait_ge(bc_rest_done, b + 1)
                nc.scalar.activation(bc_mid[2 * BC:3 * BC, b, :], bc_rest[2 * BC:3 * BC, b, :],
                                     ACT.Copy).then_inc(bc_mid_done, 1)
                nc.scalar.activation(bc_parts[BC:2 * BC, b, :], bc_rest[BC:2 * BC, b, :],
                                     ACT.Copy).then_inc(bc_mid_done, 1)

            def softplus_log(unit):
                bs = UNITS[unit]
                act.wait_ge(dt_abs_done, bs.stop)
                nc.scalar.activation(dt_abs[:, bs], dt_abs[:, bs], ACT.Exp, scale=-1.0).then_inc(dt_exp_done, 1)
                act.wait_ge(dt_exp_done, unit + 1)
                nc.scalar.activation(dt_ln[:, bs], dt_abs[:, bs], ACT.Ln, bias=1.0).then_inc(dt_ln_done, 1)

            def decays(t):
                b, g, e = t // TPB, (t % TPB) // EH, t % EH
                if t == 0:
                    act.wait_ge(a_ready, 1)
                    act.wait_ge(decay_zeroed, N_DECAY)
                if t == 0 or t == TPB:
                    act.wait_ge(delta_done, unit_end(b))
                if t >= N_DECAY:
                    act.wait_ge(scan_done, 2 * (t - N_DECAY + 1))
                for n in range(NG):
                    last = nc.scalar.activation(decay[t % N_DECAY][:, n, 1:L], delta[:, b, e, 1:L], ACT.Exp,
                                                scale=a_neg[:, e, NG * g + n:NG * g + n + 1])
                last.then_inc(decay_done, 1)

            def copy_c(grp, half):
                act.wait_ge(c_psum_done, 2 * grp + half + 1)
                if grp >= N_CREP:
                    act.wait_ge(prod_done, EH * (grp - N_CREP + 1))
                nc.scalar.activation(c_rep[grp % N_CREP][:, 2 * half:2 * half + 2, :],
                                     ps_c[:].rearrange("p (n l) -> p n l", n=2), ACT.Copy).then_inc(c_rep_done, 1)

            act.wait_ge(rows_ready, 1)
            nc.scalar.activation(pick[:], row_of3[:, :, None].to_broadcast([3 * BC, BC, P]),
                                 ACT.Copy).then_inc(pick_ready, 1)
            conv_tap(0)
            act.wait_ge(ld_g, 16)
            nc.scalar.activation(tanh_g[:], gains_sb[:], ACT.Tanh).then_inc(tanh_g_ready, 1)
            nc.scalar.activation(a_exp[:], par_sb[:, :, C_ALOG:C_ALOG + DS], ACT.Exp).then_inc(a_exp_ready, 1)
            conv_tanh(0)
            split_rows(0)
            step_size(0)
            middle_rows(0)
            softplus_log(0)
            copy_c(0, 0)
            decays(0)
            for s, steps in enumerate(slots):
                if s + 1 < NT:
                    decays(s + 1)
                if s % 2 == 0 and s < NT:
                    copy_c(s // 2, 1)
                if s % 2 == 1 and s + 1 < NT:
                    copy_c((s + 1) // 2, 0)
                for what, b, h in steps:
                    if what == "conv":
                        conv_tap(b)
                        conv_tanh(b)
                    elif what == "xdbl":
                        split_rows(b)
                        step_size(b)
                        middle_rows(b)
                    elif what == "delta":
                        softplus_log(1)
                    elif what == "norm":
                        act.wait_ge(ld_w1, 16)
                        nc.scalar.activation(w_below[:, 0:KD * H], w_up_in[:, 0], ACT.Abs,
                                             accum_out=abs_sum[:, 0:1]).then_inc(abs_done, 1)
                        act.wait_ge(ld_w2, 16)
                        act.wait_ge(abs_done, 1)
                        nc.scalar.activation(w_below[:, 0:KD * H], w_up_in[:, 1], ACT.Abs,
                                             accum_out=abs_sum[:, 1:2]).then_inc(abs_done, 1)
                        act.wait_ge(ld_w3, 16)
                        act.wait_ge(abs_done, 2)
                        nc.scalar.activation(w_below[:, 0:HF * L], w_down_in[:, 0:HF, :], ACT.Abs,
                                             accum_out=abs_sum[:, 2:3]).then_inc(abs_done, 1)
                        act.wait_ge(ld_w3l, 16)
                        act.wait_ge(abs_zeroed, 1)
                        act.wait_ge(abs_done, 3)
                        nc.scalar.activation(w_below[0:HL, 0:L], w_down_in[0:HL, HF, :], ACT.Abs,
                                             accum_out=abs_sum[0:HL, 3:4]).then_inc(abs_done, 1)
                    elif what == "gate":
                        act.wait_ge(z_half_done, EH * (b + 1))
                        act.wait_ge(u_done, NB)
                        nc.scalar.activation(z_tanh[:, b], z_half[:, b], ACT.Tanh).then_inc(z_tanh_done, 1)
                    elif what == "resid":
                        act.wait_ge(shift2_done, b + 1)
                        for t in range(KD):
                            c = KD * b + t
                            nc.scalar.activation(z2_sb[:, t, :], x1_sb[:, b % 2, t, :], ACT.Identity,
                                                 bias=shift2[:, c:c + 1],
                                                 scale=rstd2[:, c:c + 1]).then_inc(z2_done, 1)
                    elif what == "split":
                        act.wait_ge(z2_t_done, b + 1)
                        if b > 0:
                            act.wait_ge(up_done, HC * b)
                        nc.scalar.activation(z2_hi[:], ps_w1[:].rearrange("p (k l) -> p k l", k=KD),
                                             ACT.Copy).then_inc(hi_done, 1)
                        act.wait_ge(rest_done, b + 1)
                        nc.scalar.activation(z2_mid[:], z2_rest[:], ACT.Copy).then_inc(mid_done, 1)
                    elif what == "up":
                        k = HC * b + h
                        rows = P if h < HF else HL
                        act.wait_ge(up_done, k + 1)
                        if k >= 2:
                            act.wait_ge(hidden_done, k - 1)
                        nc.scalar.activation(up_tanh[0:rows, k % 2, :], up_bank(b, h)[0:rows, 0:L], ACT.Tanh,
                                             scale=0.5).then_inc(up_tanh_done, 1)

        @block.vector
        def _(dve):
            def conv_taps(b):
                dve.wait_ge(tap_done, EH * (b + 1))
                done = EH * (DC - 1) * b
                for k in range(1, DC):
                    for e in range(EH):
                        if k > 1:
                            dve.wait_ge(conv_step, done - EH + 1)
                        nc.vector.scalar_tensor_tensor(
                            out=conv[:, b, e, k:L], in0=ps_w0[:, e * L:(e + 1) * L - k],
                            scalar=half_conv[:, e, DC - 1 - k:DC - k], in1=conv[:, b, e, k:L],
                            op0=ALU.mult, op1=ALU.add).then_inc(conv_step, 1)
                        done += 1

            def silu_conv(b):
                dve.wait_ge(conv_tanh_done, b + 1)
                nc.vector.scalar_tensor_tensor(out=u_sb[:, b], in0=conv_t[:, b], scalar=1.0, in1=conv[:, b],
                                               op0=ALU.add, op1=ALU.mult).then_inc(u_done, 1)

            def rest_rows(b):
                dve.wait_ge(bc_hi_done, b + 1)
                nc.vector.tensor_tensor(bc_rest[:, b, :], ps_w1[0:3 * BC, 0:L], bc_parts[:, b, :],
                                        ALU.subtract).then_inc(bc_rest_done, 1)

            def low_rows(b):
                dve.wait_ge(bc_mid_done, 2 * b + 1)
                rows = slice(2 * BC, 3 * BC)
                nc.vector.tensor_tensor(bc_parts[rows, b, :], bc_rest[rows, b, :], bc_mid[rows, b, :],
                                        ALU.subtract).then_inc(bc_lo_done, 1)

            def softplus_sum(unit):
                bs = UNITS[unit]
                dve.wait_ge(dt_ln_done, unit + 1)
                nc.vector.scalar_tensor_tensor(out=delta[:, bs], in0=dt_x[:, bs], scalar=0.0, in1=dt_ln[:, bs],
                                               op0=ALU.max, op1=ALU.add).then_inc(delta_done, 1)

            def scan_tile(t):
                b, g, e = t // TPB, (t % TPB) // EH, t % EH
                grp = t // EH
                if t == 0 or t == TPB:
                    dve.wait_ge(du_done, unit_end(b))
                if e == 0:
                    dve.wait_ge(b_rep_done, grp + 1)
                for q in range(2):
                    if t >= 1:
                        dve.wait_ge(scan_done, 2 * (t - 1) + q + 1)
                    nc.vector.tensor_tensor(
                        ps_db[:, q * QW:(q + 1) * QW].rearrange("p (n l) -> p n l", n=2),
                        du[:, b, e, None, :].to_broadcast([P, 2, L]),
                        ps_b[:, q * QW:(q + 1) * QW].rearrange("p (n l) -> p n l", n=2),
                        ALU.mult).then_inc(db_done, 1)
                dve.wait_ge(decay_done, t + 1)
                if t >= N_STATE:
                    dve.wait_ge(prod_done, t - N_STATE + 1)
                for q in range(2):
                    dve.wait_ge(db_done, 2 * t + q + 1)
                    nc.vector.tensor_tensor_scan(
                        state[t % N_STATE][:].rearrange("p n l -> p (n l)")[:, q * QW:(q + 1) * QW],
                        decay[t % N_DECAY][:].rearrange("p n l -> p (n l)")[:, q * QW:(q + 1) * QW],
                        ps_db[:, q * QW:(q + 1) * QW], 0.0, ALU.mult, ALU.add).then_inc(scan_done, 1)

            dve.wait_ge(ld_par, 16)
            nc.vector.tensor_scalar(half_conv[:], par_sb[:, :, C_CONVW:C_CONVW + DC + 1], 0.5, None,
                                    ALU.mult).then_inc(half_conv_ready, 1)
            dve.wait_ge(ld_xw, 16)
            for k in range(3):
                nc.vector.tensor_copy(xw_sb[:, :, k * BC:(k + 1) * BC], xw_in[:, :, 0:BC]).then_inc(xw_ready, 1)
            nc.vector.tensor_copy(xw_sb[:, :, DT0:DT0 + DR], xw_in[:, :, BC:BC + DR]).then_inc(xw_ready, 1)
            for i in range(N_DECAY):
                nc.vector.memset(decay[i][:, :, 0:1], 0.0).then_inc(decay_zeroed, 1)
            dve.wait_ge(half_conv_ready, 1)
            conv_taps(0)
            dve.wait_ge(a_exp_ready, 1)
            nc.vector.tensor_scalar(a_neg[:], a_exp[:], -1.0, None, ALU.mult).then_inc(a_ready, 1)
            dve.wait_ge(tanh_g_ready, 1)
            nc.vector.tensor_scalar(half_tanh_g[:], tanh_g[:], 0.5, None, ALU.mult).then_inc(half_g_ready, 1)
            silu_conv(0)
            rest_rows(0)
            low_rows(0)
            softplus_sum(0)

            for s, steps in enumerate(slots):
                for what, b, h in steps:
                    if what == "comb":
                        dve.wait_ge(sum_done, TPB * (b + 1))
                        for e in range(EH):
                            nc.vector.scalar_tensor_tensor(
                                out=y_d[:, e, :], in0=u_sb[:, b, e, :], scalar=par_sb[:, e, C_D:C_D + 1],
                                in1=ps_y[:, e * L:(e + 1) * L], op0=ALU.mult, op1=ALU.add).then_inc(y_d_done, 1)
                        dve.wait_ge(y_d_done, EH * (b + 1))
                        dve.wait_ge(gate_done, b + 1)
                        if b > 0:
                            dve.wait_ge(mixed_t_done, b)
                        nc.vector.scalar_tensor_tensor(
                            out=mixed[:], in0=y_d[:], scalar=tanh_g[:, 0:1], in1=gate[:, b],
                            op0=ALU.mult, op1=ALU.mult).then_inc(mixed_done, 1)
                if s < NT:
                    scan_tile(s)
                for what, b, h in steps:
                    if what == "conv":
                        conv_taps(b)
                        silu_conv(b)
                    elif what == "xdbl":
                        rest_rows(b)
                        low_rows(b)
                    elif what == "delta":
                        softplus_sum(1)
                    elif what == "norm":
                        dve.wait_ge(ld_x, 16)
                        for c in range(NB * KD):
                            nc.vector.bn_stats(ln_stats[:, c, :], x_sb[:, c // KD, c % KD, :]).then_inc(stats_done, 1)
                        for c in range(NB * KD):
                            dve.wait_ge(stats_done, c + 1)
                            nc.vector.bn_aggr(ln_mv[:, c, :], ln_stats[:, c, :]).then_inc(mv_done, 1)
                        dve.wait_ge(mv_done, NB * KD)
                        nc.vector.tensor_scalar(ln_ve[:], ln_mv[:, :, 1], LN_EPS, None, ALU.add).then_inc(ve_done, 1)
                        dve.wait_ge(gamma_done, 1)
                        nc.vector.tensor_scalar(thr[:, 0:2], ps_w1[:, 0:2], 0.5 / (H * L), 0.5 * Q_EPS,
                                                ALU.mult, ALU.add).then_inc(thr_step, 1)
                        nc.vector.tensor_reduce(thr[:, 3:4], ps_w1[:, 2:4], AX_X, ALU.add).then_inc(thr_step, 1)
                        dve.wait_ge(thr_step, 2)
                        nc.vector.tensor_scalar(thr[:, 2:3], thr[:, 3:4], 0.5 / (H * L), 0.5 * Q_EPS,
                                                ALU.mult, ALU.add).then_inc(thr_step, 1)
                        dve.wait_ge(thr_step, 3)
                        nc.vector.tensor_scalar(thr_neg[:, 0:3], thr[:, 0:3], -1.0, None,
                                                ALU.mult).then_inc(thr_step, 1)
                        dve.wait_ge(rstd_done, 1)
                        nc.vector.tensor_scalar(ln_half[:], ln_rstd[:], 0.5, None, ALU.mult).then_inc(ln_half_done, 1)
                    elif what == "quant" and b < 2:
                        dve.wait_ge(thr_step, 4)
                        if b > 0:
                            dve.wait_ge(quant_done, 2 * b)
                        below = w_below[:, 0:KD * H].rearrange("p (k h) -> p k h", k=KD)
                        nc.vector.tensor_scalar(below, w_up_in[:, b], thr_neg[:, b:b + 1], None,
                                                ALU.is_lt).then_inc(below_done, 1)
                        dve.wait_ge(below_done, b + 1)
                        full, rest = HF * P, 2 * HF * P + b * HL
                        for src, dst in ((slice(0, full), slice(b * full, (b + 1) * full)),
                                         (slice(full, H), slice(rest, rest + HL))):
                            nc.vector.scalar_tensor_tensor(
                                out=w_up_q[:, :, dst], in0=w_up_in[:, b, :, src], scalar=thr[:, b:b + 1],
                                in1=below[:, :, src], op0=ALU.is_gt, op1=ALU.subtract).then_inc(quant_done, 1)
                    elif what == "quant":
                        dve.wait_ge(quant_done, 4)
                        below = w_below[:, 0:HC * L].rearrange("p (c d) -> p c d", c=HC)
                        for rows, cs in ((P, slice(0, HF)), (HL, slice(HF, HC))):
                            nc.vector.tensor_scalar(below[0:rows, cs], w_down_in[0:rows, cs], thr_neg[0:rows, 2:3],
                                                    None, ALU.is_lt).then_inc(below_done, 1)
                        dve.wait_ge(below_done, 4)
                        for rows, cs in ((P, slice(0, HF)), (HL, slice(HF, HC))):
                            nc.vector.scalar_tensor_tensor(
                                out=w_down_q[0:rows, cs], in0=w_down_in[0:rows, cs], scalar=thr[0:rows, 2:3],
                                in1=below[0:rows, cs], op0=ALU.is_gt, op1=ALU.subtract).then_inc(quant_done, 1)
                    elif what == "gate":
                        dve.wait_ge(ln_half_done, 1)
                        dve.wait_ge(delta_done, 2)
                        for e in range(EH):
                            c = KD * b + e
                            nc.vector.tensor_scalar(z_half[:, b, e, :], x_sb[:, b, e, :], ln_mv[:, c, 0:1],
                                                    ln_half[:, c:c + 1], ALU.subtract,
                                                    ALU.mult).then_inc(z_half_done, 1)
                        dve.wait_ge(z_tanh_done, b + 1)
                        nc.vector.scalar_tensor_tensor(out=gate[:, b], in0=z_tanh[:, b], scalar=1.0,
                                                       in1=z_half[:, b], op0=ALU.add,
                                                       op1=ALU.mult).then_inc(gate_done, 1)
                    elif what == "resid":
                        dve.wait_ge(mixed_t_done, b + 1)
                        nc.vector.tensor_tensor(x1_sb[:, b % 2], x_sb[:, b],
                                                ps_w0[:].rearrange("p (t l) -> p t l", t=KD),
                                                ALU.add).then_inc(x1_done, 1)
                        dve.wait_ge(x1_done, b + 1)
                        for t in range(KD):
                            nc.vector.bn_stats(st2[:, KD * b + t, :], x1_sb[:, b % 2, t, :]).then_inc(st2_done, 1)
                        for t in range(KD):
                            dve.wait_ge(st2_done, KD * b + t + 1)
                            nc.vector.bn_aggr(mv2[:, KD * b + t, :], st2[:, KD * b + t, :]).then_inc(mv2_done, 1)
                        dve.wait_ge(mv2_done, KD * (b + 1))
                        c = slice(KD * b, KD * b + KD)
                        nc.vector.tensor_scalar(ve2[:, c], mv2[:, c, 1], LN_EPS, None, ALU.add).then_inc(ve2_done, 1)
                        dve.wait_ge(rstd2_done, b + 1)
                        nc.vector.scalar_tensor_tensor(out=shift2[:, c], in0=mv2[:, c, 0], scalar=-1.0,
                                                       in1=rstd2[:, c], op0=ALU.mult,
                                                       op1=ALU.mult).then_inc(shift2_done, 1)
                    elif what == "split":
                        dve.wait_ge(hi_done, b + 1)
                        nc.vector.tensor_tensor(z2_rest[:], ps_w1[:].rearrange("p (k l) -> p k l", k=KD),
                                                z2_hi[:], ALU.subtract).then_inc(rest_done, 1)
                    elif what == "up":
                        k = HC * b + h
                        rows = P if h < HF else HL
                        dve.wait_ge(up_tanh_done, k + 1)
                        if b >= 2 and h == 0:
                            dve.wait_ge(down_done, b - 1)
                        x2 = up_bank(b, h)[:, L:2 * L] if h < HF else up_bank(b, h)[HL:2 * HL, 0:L]
                        nc.vector.scalar_tensor_tensor(out=hidden[0:rows, b % 2, h, :],
                                                       in0=up_tanh[0:rows, k % 2, :], scalar=1.0, in1=x2,
                                                       op0=ALU.add, op1=ALU.mult).then_inc(hidden_done, 1)
                    elif what == "out":
                        dve.wait_ge(down_done, b + 1)
                        for t in range(KD):
                            nc.vector.scalar_tensor_tensor(
                                out=x_sb[:, b, t, :], in0=ps_w1[:, t * L:(t + 1) * L],
                                scalar=half_tanh_g[:, 1:2], in1=x1_sb[:, b % 2, t, :],
                                op0=ALU.mult, op1=ALU.add).then_inc(out_done, 1)

        @block.tensor
        def _(pe):
            def project_in(b):
                pe.wait_ge(ld_ctx0 if b == 0 else ld_ctx, 16)
                if b > 0:
                    pe.wait_ge(dt_x_done, EH * b)
                for e in range(EH):
                    last = nc.tensor.matmul(ps_w0[:, e * L:(e + 1) * L], win_sb[:, e * P:(e + 1) * P],
                                            ctx_sb[:, b, :], start=True, stop=True)
                last.then_inc(in_done, 1)

            def rows_bc_dt(b):
                pe.wait_ge(u_done, b + 1)
                if b == 0:
                    pe.wait_ge(xw_ready, 4)
                else:
                    pe.wait_ge(bc_rest_done, b)
                for e in range(EH):
                    last = nc.tensor.matmul(ps_w1[0:DT0 + DR, 0:L], xw_sb[:, e, :], u_sb[:, b, e, :],
                                            start=(e == 0), stop=(e == EH - 1))
                last.then_inc(rows_done, 1)
                if b == 0:
                    pe.wait_ge(ld_dtw, 16)
                pe.wait_ge(dt_low_done, b + 1)
                for e in range(EH):
                    last = nc.tensor.matmul(ps_w0[:, e * L:(e + 1) * L], dtw_sb[DT0:DT0 + DR, e * P:(e + 1) * P],
                                            dt_low[DT0:DT0 + DR, b, :], start=True, stop=True)
                last.then_inc(dt_done, 1)

            def spread_b(grp):
                b, g = grp // NGRP, grp % NGRP
                if g == 0:
                    pe.wait_ge(bc_mid_done, 2 * (b + 1))
                    pe.wait_ge(bc_lo_done, b + 1)
                if grp == 0:
                    pe.wait_ge(pick_ready, 1)
                else:
                    pe.wait_ge(db_done, 2 * EH * grp)
                for n in range(NG):
                    last = nc.tensor.matmul(ps_b[:, n * L:(n + 1) * L], pick[:, NG * g + n, :],
                                            bc_parts[:, b, :], start=True, stop=True)
                last.then_inc(b_rep_done, 1)

            def spread_c(grp, half):
                b, g = grp // NGRP, grp % NGRP
                if g == 0 and half == 0:
                    pe.wait_ge(bc_mid_done, 2 * (b + 1))
                    pe.wait_ge(bc_lo_done, b + 1)
                if grp > 0 or half > 0:
                    pe.wait_ge(c_rep_done, 2 * grp + half)
                for n in range(2):
                    last = nc.tensor.matmul(ps_c[:, n * L:(n + 1) * L], pick[:, DS + NG * g + 2 * half + n, :],
                                            bc_parts[:, b, :], start=True, stop=True)
                last.then_inc(c_psum_done, 1)

            def sum_states(t):
                b, g, e = t // TPB, (t % TPB) // EH, t % EH
                pe.wait_ge(prod_done, t + 1)
                if t % TPB == 0 and b > 0:
                    pe.wait_ge(y_d_done, EH * b)
                for n in range(NG):
                    last = nc.tensor.matmul(ps_y[:, e * L:(e + 1) * L], ident[:], prod[t % N_PROD][:, n, :],
                                            start=(t % TPB == 0 and n == 0),
                                            stop=(t % TPB == TPB - 1 and n == NG - 1), skip_group_check=True)
                last.then_inc(sum_done, 1)

            pe.wait_ge(ld_win, 16)
            project_in(0)
            rows_bc_dt(0)
            spread_c(0, 0)
            for s, steps in enumerate(slots):
                if s == 0:
                    spread_b(0)
                if s % 2 == 0 and s < NT:
                    if s > 0:
                        spread_b(s // 2)
                    spread_c(s // 2, 1)
                if s == 0:
                    pe.wait_ge(ident_ready, 1)
                if LAG <= s < NT + LAG:
                    sum_states(s - LAG)
                if s % 2 == 1 and s + 1 < NT:
                    spread_c((s + 1) // 2, 0)
                for what, b, h in steps:
                    if what == "conv":
                        project_in(b)
                    elif what == "xdbl":
                        rows_bc_dt(b)
                    elif what == "norm":
                        pe.wait_ge(abs_done, 4)
                        pe.wait_ge(const_ready, 2)
                        pe.wait_ge(bc_rest_done, NB)
                        nc.tensor.matmul(ps_w1[:, 0:4], ones[:], abs_sum[:], start=True,
                                         stop=True).then_inc(gamma_done, 1)
                    elif what == "resid":
                        pe.wait_ge(mixed_done, b + 1)
                        pe.wait_ge(dt_x_done, EH * NB) if b == 0 else pe.wait_ge(hidden_done, HC * b)
                        for t in range(KD):
                            for e in range(EH):
                                last = nc.tensor.transpose(ps_w0[:, t * L + e * P:t * L + (e + 1) * P],
                                                           mixed[:, e, t * P:(t + 1) * P], ident[:])
                        last.then_inc(mixed_t_done, 1)
                    elif what == "split":
                        pe.wait_ge(z2_done, KD * (b + 1))
                        pe.wait_ge(thr_step, 2) if b == 0 else pe.wait_ge(out_done, KD * b)
                        for k in range(KD):
                            for t in range(KD):
                                last = nc.tensor.transpose(ps_w1[:, k * L + t * P:k * L + (t + 1) * P],
                                                           z2_sb[:, t, k * P:(k + 1) * P], ident[:])
                        last.then_inc(z2_t_done, 1)
                    elif what == "up":
                        k = HC * b + h
                        if h == 0:
                            pe.wait_ge(lo_done, b + 1)
                            pe.wait_ge(x1_done, b + 1)
                            pe.wait_ge(quant_done, 4)
                        if b < NB - 1 and h > 0:
                            pe.wait_ge(hidden_done, k)
                        elif b == NB - 1 and h > 1:
                            pe.wait_ge(hidden_done, k - 1)
                        bank = up_bank(b, h)
                        if h < HF:
                            cols = ((h * P, slice(0, L)), ((HF + h) * P, slice(L, 2 * L)))
                        else:
                            cols = ((2 * HF * P, slice(0, L)),)
                        for i, (at, where) in enumerate(cols):
                            parts = [(z, kd) for z in (z2_hi, z2_mid, z2_lo) for kd in range(KD)]
                            for j, (z, kd) in enumerate(parts):
                                last = nc.tensor.matmul(bank[:, where], w_up_q[:, kd, at:at + P], z[:, kd, :],
                                                        start=(i == 0 and j == 0),
                                                        stop=(i == len(cols) - 1 and j == len(parts) - 1),
                                                        skip_group_check=True)
                        last.then_inc(up_done, 1)
                    elif what == "down":
                        rows = P if h < HF else HL
                        pe.wait_ge(hidden_done, HC * b + h + 1)
                        if h == 0:
                            pe.wait_ge(quant_done, 6)
                            pe.wait_ge(rest_done, b + 1)
                        for t in range(KD):
                            last = nc.tensor.matmul(ps_w1[:, t * L:(t + 1) * L],
                                                    hidden[0:rows, b % 2, h, t * P:(t + 1) * P],
                                                    w_down_q[0:rows, h, :], start=(h == 0 and t == 0),
                                                    stop=(h == HC - 1 and t == KD - 1), skip_group_check=True)
                        if h == HC - 1:
                            last.then_inc(down_done, 1)


def kernel(**inputs):
    import numpy as np
    import concourse.bacc as bacc
    from concourse.bass_utils import run_bass_kernel_spmd

    a = {k: np.asarray(v) for k, v in inputs.items()}
    pre = "L0_xattn_"
    xw = a[pre + "x_proj_w"]
    arrays = {
        "x": a["x"],
        "ctxT": a["ctx_1024"].transpose(2, 0, 1),
        "gains": np.concatenate([a["g_xattn"], a["g_ffn"]]),
        "winT": a[pre + "in_proj_w"].T,
        "par": np.concatenate([a[pre + "conv_w"], a[pre + "conv_b"][:, None], a[pre + "dt_proj_b"][:, None],
                               a[pre + "A_log"], a[pre + "D"][:, None]], axis=1),
        "xwT": np.concatenate([xw[DR:], xw[:DR]], axis=0).T,
        "dtwT": a[pre + "dt_proj_w"].T,
        "w1T": a["L0_ffn_w1"].T,
        "w2T": a["L0_ffn_w2"].T,
        "w3T": a["L0_ffn_w3"].T,
    }
    nc = bacc.Bacc("TRN2", target_bir_lowering=False, num_devices=1)
    ins, args = {}, []
    for name, v in arrays.items():
        v = np.ascontiguousarray(v)
        ins[f"in_{name}"] = v
        args.append(nc.dram_tensor(f"in_{name}", v.shape, mybir.dt.from_np(v.dtype), kind="ExternalInput").ap())
    out = nc.dram_tensor("out_0", (NB, L, L), F32, kind="ExternalOutput").ap()
    gated_ssm_ffn_kernel(nc, *args, out)
    r = run_bass_kernel_spmd(nc, [ins], core_ids=[0])
    return r.results[0]["out_0"]
```

```python
from contextlib import ExitStack

import concourse.bass as bass
from concourse import mybir

F32 = mybir.dt.float32
BF16 = mybir.dt.bfloat16
ALU = mybir.AluOpType
ACT = mybir.ActivationFunctionType
AX_X = mybir.AxisListType.X

P = 128
NB = 4
L = 256
DM = 128
DI = 256
EH = DI // P
DS = 16
DR = 8
DC = 4
H = 704
HC = 6
HF = H // P
HL = H - HF * P
KD = L // P
NG = 4
NGRP = DS // NG
TPB = NGRP * EH
NT = NB * TPB
QW = 512
LN_EPS = 1e-5
Q_EPS = 1e-8

N_DECAY = 3
N_STATE = 4
N_PROD = 4
N_CREP = 3
N_WARM = 8
LAG = 2

HALVED = [0, 1, 2, 5, 6, 7, 12, 15, 17, 19, 21, 23, 25, 26, 27, 29, 30, 31]

BEFORE, MIDDLE, AFTER = range(3)

C_CONVB, C_DTB, C_ALOG, C_D = 0, 1, 2, 2 + DS
NPAR = C_D + 1
BC = 2 * DS
DT0 = 3 * BC


PLAN = [
    (0, BEFORE, [("conv", 1, 0), ("conv", 2, 0)]),
    (1, AFTER, [("conv", 3, 0), ("stats", 0, 0), ("stats", 1, 0), ("rstd", 0, 0)]),
    (2, MIDDLE, [("silu_conv", 1, 0)]),
    (2, AFTER, [("silu_conv", 2, 0)]),
    (3, MIDDLE, [("conv_tanh", 1, 0), ("conv_tanh", 2, 0), ("conv_tanh", 3, 0), ("silu_conv", 3, 0)]),
    (3, AFTER, [("rows", 1, 0)]),
    (4, MIDDLE, [("abs_w", 0, 0)]),
    (4, AFTER, [("rest_rows", 1, 0)]),
    (5, MIDDLE, [("rows", 2, 0), ("split_rows", 1, 0)]),
    (5, AFTER, [("dt", 1, 0), ("low_rows", 1, 0)]),
    (6, MIDDLE, [("rows", 3, 0), ("mid_rows", 1, 0), ("abs_w", 1, 0), ("split_rows", 2, 0),
                 ("abs_dt", 1, 0), ("abs_w", 2, 0), ("relu_dt", 1, 0), ("mid_rows", 2, 0),
                 ("split_rows", 3, 0), ("abs_dt", 2, 0), ("z_half", 0, 0), ("relu_dt", 2, 0),
                 ("z_tanh", 0, 0), ("mid_rows", 3, 0), ("abs_dt", 3, 0), ("softplus_log", 1, 0),
                 ("relu_dt", 3, 0)]),
    (6, AFTER, [("rest_rows", 2, 0)]),
    (7, MIDDLE, [("dt", 2, 0)]),
    (7, AFTER, [("gamma", 0, 0), ("low_rows", 2, 0), ("ln_shift", 0, 0), ("rest_rows", 3, 0),
                ("thresholds", 0, 0), ("quant", 0, 0), ("low_rows", 3, 0), ("gate", 0, 0), ("quant", 1, 0),
                ("mix", 0, 0), ("quant", 2, 0), ("softplus_sum", 1, 0), ("delta_u", 1, 0),
                ("softplus_sum", 2, 0), ("delta_u", 2, 0), ("softplus_sum", 3, 0)]),
    (8, MIDDLE, [("dt", 3, 0), ("rstd2", 0, 0), ("delta_u", 3, 0)]),
    (8, AFTER, [("x1", 0, 0)]),
    (9, MIDDLE, [("mix_t", 0, 0)]),
    (9, AFTER, [("shift2", 0, 0)]),
    (10, MIDDLE, [("z2_t", 0, 0), ("z_half", 1, 0), ("z_half", 2, 0), ("z2", 0, 0)]),
    (11, MIDDLE, [("z_tanh", 1, 0)]),
    (12, MIDDLE, [("z2_hi", 0, 0), ("z2_rest", 0, 0)]),
    (12, AFTER, [("z2_lo", 0, 0)]),
    (13, MIDDLE, [("up", 0, 0), ("z2_mid", 0, 0), ("z_half", 3, 0)]),
    (13, AFTER, [("up", 0, 1), ("hidden", 0, 0)]),
    (14, MIDDLE, [("up", 0, 2), ("up_tanh", 0, 0)]),
    (14, AFTER, [("hidden", 0, 1)]),
    (15, MIDDLE, [("up_tanh", 0, 1)]),
    (15, AFTER, [("hidden", 0, 2)]),
    (16, MIDDLE, [("up", 0, 3), ("down", 0, 0), ("up_tanh", 0, 2)]),
    (17, MIDDLE, [("gate", 1, 0)]),
    (17, AFTER, [("down", 0, 1), ("up", 0, 4), ("mix", 1, 0)]),
    (18, MIDDLE, [("mix_t", 1, 0), ("up_tanh", 0, 3), ("z_tanh", 2, 0), ("hidden", 0, 3), ("rstd2", 1, 0)]),
    (18, AFTER, [("hidden", 0, 4)]),
    (19, MIDDLE, [("up_tanh", 0, 4), ("x1", 1, 0)]),
    (19, AFTER, [("shift2", 1, 0)]),
    (20, MIDDLE, [("up", 0, 5), ("down", 0, 2), ("down", 0, 3), ("z2_t", 1, 0), ("z2", 1, 0),
                  ("up_tanh", 0, 5)]),
    (20, AFTER, [("hidden", 0, 5)]),
    (21, AFTER, [("down", 0, 4), ("z2_rest", 1, 0)]),
    (22, MIDDLE, [("down", 0, 5), ("up", 1, 0), ("z2_hi", 1, 0)]),
    (22, AFTER, [("z2_lo", 1, 0)]),
    (23, MIDDLE, [("z2_mid", 1, 0)]),
    (23, AFTER, [("up", 1, 1), ("hidden", 1, 0), ("gate", 2, 0)]),
    (24, MIDDLE, [("up", 1, 2), ("up_tanh", 1, 0), ("hidden", 1, 1)]),
    (24, AFTER, [("out", 0, 0)]),
    (25, MIDDLE, [("up", 1, 3), ("up_tanh", 1, 1), ("z_tanh", 3, 0), ("hidden", 1, 2)]),
    (25, AFTER, [("up", 1, 4), ("down", 1, 0), ("up", 1, 5), ("hidden", 1, 3)]),
    (26, MIDDLE, [("mix_t", 2, 0), ("up_tanh", 1, 2), ("up_tanh", 1, 3), ("mix", 2, 0), ("hidden", 1, 4)]),
    (26, AFTER, [("hidden", 1, 5)]),
    (27, MIDDLE, [("up_tanh", 1, 4), ("up_tanh", 1, 5), ("rstd2", 2, 0)]),
    (27, AFTER, [("down", 1, 1), ("x1", 2, 0)]),
    (28, MIDDLE, [("down", 1, 2), ("down", 1, 3), ("down", 1, 4)]),
    (28, AFTER, [("shift2", 2, 0)]),
    (29, MIDDLE, [("z2_t", 2, 0), ("z2", 2, 0)]),
    (29, AFTER, [("down", 1, 5), ("z2_rest", 2, 0)]),
    (30, MIDDLE, [("up", 2, 0), ("z2_hi", 2, 0), ("z2_mid", 2, 0), ("up_tanh", 2, 0), ("up_tanh", 2, 1),
                  ("up_tanh", 2, 2), ("up_tanh", 2, 3), ("up_tanh", 2, 4), ("up_tanh", 2, 5),
                  ("z2_hi", 3, 0), ("z2_mid", 3, 0), ("up_tanh", 3, 0), ("up_tanh", 3, 1),
                  ("up_tanh", 3, 2), ("up_tanh", 3, 3), ("up_tanh", 3, 4), ("up_tanh", 3, 5),
                  ("z2_lo", 2, 0)]),
    (31, MIDDLE, [("up", 2, 1), ("up", 2, 2), ("hidden", 2, 0)]),
    (31, AFTER, [("out", 1, 0), ("gate", 3, 0), ("hidden", 2, 1), ("hidden", 2, 2), ("hidden", 2, 3),
                 ("mix", 3, 0), ("x1", 3, 0), ("hidden", 2, 4), ("shift2", 3, 0), ("z2", 3, 0),
                 ("hidden", 2, 5), ("z2_rest", 3, 0), ("z2_lo", 3, 0), ("out", 2, 0), ("hidden", 3, 0),
                 ("hidden", 3, 1), ("hidden", 3, 2), ("hidden", 3, 3), ("hidden", 3, 4), ("hidden", 3, 5),
                 ("out", 3, 0), ("rstd2", 3, 0)]),
    (32, MIDDLE, [("up", 2, 3), ("down", 2, 0), ("mix_t", 3, 0), ("up", 2, 4), ("down", 2, 1),
                  ("up", 2, 5), ("down", 2, 2), ("z2_t", 3, 0), ("down", 2, 3), ("down", 2, 4),
                  ("down", 2, 5), ("up", 3, 0), ("up", 3, 1), ("down", 3, 0), ("up", 3, 2), ("down", 3, 1),
                  ("up", 3, 3), ("down", 3, 2), ("up", 3, 4), ("down", 3, 3), ("up", 3, 5), ("down", 3, 4),
                  ("down", 3, 5)]),
]


def schedule():
    lists = [[[] for _ in range(NT + 20)] for _ in range(3)]
    for slot, place, steps in PLAN:
        lists[place][slot] += steps
    return lists


def gated_ssm_ffn_kernel(nc, x, ctxT, gains, winT, convT, par, xwT, dtwT, w1T, w2T, w3T, c_rows, out):
    before, middle, after = schedule()
    with ExitStack() as es:
        def sb(name, shape, dt=F32):
            return es.enter_context(nc.sbuf_tensor(name, shape, dt))

        def psum(name, cols):
            return es.enter_context(nc.psum_tensor(name, [P, cols], F32))

        def sem(name):
            return es.enter_context(nc.semaphore(name))

        par_sb = sb("par_sb", [P, EH, NPAR])
        half_conv_b = sb("half_conv_b", [P, EH, 1])
        conv_rep = sb("conv_rep", [P, DC, DI])
        win_tap = sb("win_tap", [P, DC, DI])
        a_neg = sb("a_neg", [P, EH, DS])
        a_exp = sb("a_exp", [P, EH, DS])
        gains_sb = sb("gains_sb", [P, 2])
        tanh_g = sb("tanh_g", [P, 2])
        half_tanh_g = sb("half_tanh_g", [P, 2])
        win_sb = sb("win_sb", [P, DI])
        ctx_sb = sb("ctx_sb", [P, NB, L])
        xw_in = sb("xw_in", [P, EH, BC + DR])
        xw_sb = sb("xw_sb", [P, EH, DT0 + DR])
        dtw_sb = sb("dtw_sb", [P, DI])
        x_sb = sb("x_sb", [P, NB, KD, L])
        w_up_in = sb("w_up_in", [P, 2, KD, H])
        w_down_in = sb("w_down_in", [P, HC, L])
        w_below = sb("w_below", [P, HC * L], BF16)
        w_up_q = sb("w_up_q", [P, KD, 2 * H], BF16)
        w_down_q = sb("w_down_q", [P, HC, L])
        abs_sum = sb("abs_sum", [P, 4])
        thr = sb("thr", [P, 4])
        thr_neg = sb("thr_neg", [P, 4])
        ident = sb("ident", [P, P])
        diag_d = sb("diag_d", [P, EH, P])
        ones = sb("ones", [P, P])
        zeros = sb("zeros", [P, QW], BF16)
        row_of3 = sb("row_of3", [3 * BC, BC], BF16)
        pick = sb("pick", [3 * BC, DS, P], BF16)

        conv = sb("conv", [P, NB, EH, L])
        u_sb = sb("u_sb", [P, NB, EH, L])
        dt_low = sb("dt_low", [P, 2, L])
        bc_parts = sb("bc_parts", [3 * BC, NB, L], BF16)
        bc_rest = sb("bc_rest", [3 * BC, 2, L])
        bc_rows = sb("bc_rows", [BC, 2, L])
        bc_mid = sb("bc_mid", [3 * BC, NB, L], BF16)
        dt_x = sb("dt_x", [P, NB, EH, L])
        dt_abs = conv
        dt_ln = sb("dt_ln", [P, NB, EH, L])
        delta = sb("delta", [P, NB, EH, L])
        du = sb("du", [P, NB, EH, L])

        decay = [sb(f"decay{i}", [P, NG, L]) for i in range(N_DECAY)]
        state = [sb(f"state{i}", [P, NG, L]) for i in range(N_STATE)]
        prod = [sb(f"prod{i}", [P, NG, L]) for i in range(N_PROD)]
        c_rep = [sb(f"c_rep{i}", [P, NG, L]) for i in range(N_CREP)]

        ln_stats = sb("ln_stats", [P, NB * KD, 6])
        ln_mv = sb("ln_mv", [P, NB * KD, 2])
        ln_ve = sb("ln_ve", [P, NB * KD])
        ln_half = sb("ln_half", [P, NB * KD])
        ln_rstd = sb("ln_rstd", [P, NB * KD])
        ln_shift = sb("ln_shift", [P, NB * KD])
        minus_half = sb("minus_half", [P, NB * KD])
        z_half, gate = dt_x, dt_ln
        z_tanh = sb("z_tanh", [P, EH, L])

        mixed = sb("mixed", [P, EH, L])
        x1_sb = conv_rep[:].rearrange("p (b t) l -> p b t l", b=2)
        st2 = sb("st2", [P, NB * KD, 6])
        mv2 = sb("mv2", [P, NB * KD, 2])
        ve2 = sb("ve2", [P, NB * KD])
        rstd2 = sb("rstd2", [P, NB * KD])
        shift2 = sb("shift2", [P, NB * KD])
        z2_sb = sb("z2_sb", [P, KD, L])
        z2_hi = sb("z2_hi", [P, KD, L], BF16)
        z2_rest = sb("z2_rest", [P, KD, L])
        z2_mid = sb("z2_mid", [P, KD, L], BF16)
        z2_lo = sb("z2_lo", [P, KD, L], BF16)
        up_tanh = sb("up_tanh", [P, 2, L])
        hidden = sb("hidden", [P, 2, HC, L])

        ps_b = psum("ps_b", 2 * QW)
        ps_db = psum("ps_db", 2 * QW)
        ps_t = psum("ps_t", QW)
        ps_y = psum("ps_y", QW)
        ps_w0 = psum("ps_w0", QW)
        ps_w1 = psum("ps_w1", QW)

        ld_par, ld_win, ld_ctx0, ld_ctx, ld_xw, ld_dtw = (sem(n) for n in (
            "ld_par", "ld_win", "ld_ctx0", "ld_ctx", "ld_xw", "ld_dtw"))
        ld_g, ld_x, ld_w1, ld_w2, ld_w3, ld_w3l = (sem(n) for n in (
            "ld_g", "ld_x", "ld_w1", "ld_w2", "ld_w3", "ld_w3l"))
        ident_ready, rows_ready, const_ready = sem("ident_ready"), sem("rows_ready"), sem("const_ready")
        pool_init = sem("pool_init")
        pick_ready = sem("pick_ready")
        c_loaded = [sem(f"c_loaded{i}") for i in range(N_CREP)]
        half_conv_b_ready, a_exp_ready, a_ready = sem("half_conv_b_ready"), sem("a_exp_ready"), sem("a_ready")
        last_prod_done = sem("last_prod_done")
        zeros_ready, prod_half_done = sem("zeros_ready"), sem("prod_half_done")
        xw_ready, decay_zeroed = sem("xw_ready"), sem("decay_zeroed")
        tanh_g_ready, half_g_ready = sem("tanh_g_ready"), sem("half_g_ready")
        ld_conv, ld_conv1 = sem("ld_conv"), sem("ld_conv1")
        win_tap_ready, conv_done = sem("win_tap_ready"), sem("conv_done")
        gate_step = sem("gate_step")
        conv_tanh_done, u_done = sem("conv_tanh_done"), sem("u_done")
        rows_done, dt_low_done, bc_hi_done = sem("rows_done"), sem("dt_low_done"), sem("bc_hi_done")
        bc_rest_done, bc_mid_done, bc_lo_done = sem("bc_rest_done"), sem("bc_mid_done"), sem("bc_lo_done")
        dt_done, dt_relu_done, dt_abs_done = sem("dt_done"), sem("dt_relu_done"), sem("dt_abs_done")
        dt_exp_done, dt_ln_done = sem("dt_exp_done"), sem("dt_ln_done")
        delta_done, du_done = sem("delta_done"), sem("du_done")
        b_rep_done, bc_rows_done, c_stored = sem("b_rep_done"), sem("bc_rows_done"), sem("c_stored")
        decay_done, db_done, scan_done = sem("decay_done"), sem("db_done"), sem("scan_done")
        prod_done, sum_done = sem("prod_done"), sem("sum_done")
        abs_zeroed, abs_done, gamma_done = sem("abs_zeroed"), sem("abs_done"), sem("gamma_done")
        thr_step, below_done, quant_done = sem("thr_step"), sem("below_done"), sem("quant_done")
        stats_done, mv_done, ve_done = sem("stats_done"), sem("mv_done"), sem("ve_done")
        rstd_done, ln_half_done = sem("rstd_done"), sem("ln_half_done")
        z_half_done, z_tanh_done, gate_done = sem("z_half_done"), sem("z_tanh_done"), sem("gate_done")
        diag_d_ready, mixed_done, mixed_t_done = sem("diag_d_ready"), sem("mixed_done"), sem("mixed_t_done")
        x1_done, st2_done, mv2_done = sem("x1_done"), sem("st2_done"), sem("mv2_done")
        ve2_done, rstd2_done, shift2_done = sem("ve2_done"), sem("rstd2_done"), sem("shift2_done")
        z2_done, z2_t_done, hi_done = sem("z2_done"), sem("z2_t_done"), sem("hi_done")
        rest_done, mid_done, lo_done = sem("rest_done"), sem("mid_done"), sem("lo_done")
        up_done, up_tanh_done, hidden_done = sem("up_done"), sem("up_tanh_done"), sem("hidden_done")
        down_done, out_done, stored = sem("down_done"), sem("out_done"), sem("stored")

        def conv_bank(b, e):
            return ((ps_w0, ps_db), (ps_y, ps_y), (ps_w0, ps_w0), (ps_w1, ps_w1))[b][e]

        def up_bank(h):
            return ps_t if h % 2 else ps_w0

        block = es.enter_context(nc.Block())

        @block.sync
        def _(sp):
            sp.dma_start(conv_rep[:, :, 0:P], convT[:, 0:P].partition_broadcast(P)).then_inc(ld_conv, 16)
            sp.dma_start(win_sb[:], winT).then_inc(ld_win, 16)
            sp.dma_start(ctx_sb[:, 0, :], ctxT[:, 0, :]).then_inc(ld_ctx0, 16)
            sp.dma_start(conv_rep[:, :, P:DI], convT[:, P:DI].partition_broadcast(P)).then_inc(ld_conv1, 16)
            sp.dma_start(par_sb[:], par.rearrange("(h p) c -> p h c", p=P)).then_inc(ld_par, 16)
            sp.dma_start(ctx_sb[:, 1:NB, :], ctxT[:, 1:NB, :]).then_inc(ld_ctx, 16)
            sp.dma_start(xw_in[:], xwT.rearrange("(h p) c -> p h c", p=P)).then_inc(ld_xw, 16)
            sp.dma_start(dtw_sb[DT0:DT0 + DR, :], dtwT).then_inc(ld_dtw, 16)
            sp.dma_start(x_sb[:], x.rearrange("b (t p) d -> p b t d", p=P)).then_inc(ld_x, 16)
            sp.dma_start(gains_sb[:], gains.partition_broadcast(P)).then_inc(ld_g, 16)
            sp.dma_start(w_up_in[:, 0], w1T.rearrange("(k p) h -> p k h", p=P)).then_inc(ld_w1, 16)
            sp.dma_start(w_up_in[:, 1], w2T.rearrange("(k p) h -> p k h", p=P)).then_inc(ld_w2, 16)
            sp.dma_start(w_down_in[:, 0:HF, :],
                         w3T[0:HF * P, :].rearrange("(c p) d -> p c d", p=P)).then_inc(ld_w3, 16)
            sp.dma_start(w_down_in[0:HL, HF, :], w3T[HF * P:H, :]).then_inc(ld_w3l, 16)

            def load_c(grp):
                b, g = grp // NGRP, grp % NGRP
                if g == 0:
                    sp.wait_ge(c_stored, 16 * (b + 1))
                if grp >= N_CREP:
                    sp.wait_ge(prod_done, EH * (grp - N_CREP + 1))
                sp.dma_start(c_rep[grp % N_CREP][:], c_rows[b, NG * g:NG * (g + 1), :].partition_broadcast(P)
                             ).then_inc(c_loaded[grp % N_CREP], 16)

            def store(b):
                for t in range(KD):
                    sp.wait_ge(out_done, KD * b + t + 1)
                    sp.dma_start(out[b, t * P:(t + 1) * P, :], x_sb[:, b, t, :]).then_inc(stored, 16)

            for grp in range(NB * NGRP):
                load_c(grp)
                if grp == NB * NGRP - 3:
                    store(0)
            for b in range(1, NB):
                store(b)
            sp.wait_ge(stored, 16 * NB * KD)

        @block.gpsimd
        def _(pool):
            nc.gpsimd.memset(ident[:], 0.0).then_inc(pool_init, 1)
            nc.gpsimd.memset(row_of3[:], 0.0).then_inc(pool_init, 1)
            pool.wait_ge(pool_init, 2)
            nc.gpsimd.affine_select(out=row_of3[:], in_=row_of3[:], compare_op=ALU.not_equal, fill=1.0,
                                    base=0, pattern=[[-1, BC]], channel_multiplier=1).then_inc(pool_init, 1)
            for k in range(1, 3):
                pool.wait_ge(pool_init, 2 + k)
                nc.gpsimd.affine_select(out=row_of3[:], in_=row_of3[:], compare_op=ALU.not_equal, fill=1.0,
                                        base=-BC * k, pattern=[[-1, BC]],
                                        channel_multiplier=1).then_inc(rows_ready if k == 2 else pool_init, 1)
            nc.gpsimd.affine_select(out=ident[:], in_=ident[:], compare_op=ALU.not_equal, fill=1.0,
                                    base=0, pattern=[[-1, P]], channel_multiplier=1).then_inc(ident_ready, 1)
            nc.gpsimd.memset(ones[:], 1.0).then_inc(const_ready, 1)
            nc.gpsimd.memset(minus_half[:], -0.5).then_inc(const_ready, 1)
            nc.gpsimd.memset(abs_sum[:, 3:4], 0.0).then_inc(abs_zeroed, 1)

            def product(t):
                states = slice(0, NG if t < NT - 1 else NG // 2)
                pool.wait_ge(scan_done, 2 * (t + 1) if t < NT - 1 else 2 * t + 1)
                pool.wait_ge(c_loaded[(t // EH) % N_CREP], 16 * (t // EH // N_CREP + 1))
                if t >= N_PROD:
                    pool.wait_ge(sum_done, t - N_PROD + 1)
                nc.gpsimd.tensor_tensor(prod[t % N_PROD][:, states], state[t % N_STATE][:, states],
                                        c_rep[(t // EH) % N_CREP][:, states], ALU.mult).then_inc(prod_done, 1)

            def halve(t):
                pool.wait_ge(prod_done, t + 1)
                if t == NT - 1:
                    pool.wait_ge(last_prod_done, 1)
                nc.gpsimd.tensor_tensor(prod[t % N_PROD][:, 0:2, :], prod[t % N_PROD][:, 0:2, :],
                                        prod[t % N_PROD][:, 2:4, :], ALU.add).then_inc(prod_half_done, 1)

            def own_steps(steps):
                for what, b, h in steps:
                    if what == "delta_u":
                        pool.wait_ge(delta_done, EH * (b + 1))
                        nc.gpsimd.tensor_tensor(du[:, b], delta[:, b], u_sb[:, b], ALU.mult).then_inc(du_done, EH)
                    elif what == "softplus_sum":
                        pool.wait_ge(dt_ln_done, EH * (b + 1))
                        pool.wait_ge(dt_relu_done, EH * (b + 1))
                        nc.gpsimd.tensor_tensor(delta[:, b], dt_x[:, b], dt_ln[:, b],
                                                ALU.add).then_inc(delta_done, EH)
                    elif what == "diag_d":
                        pool.wait_ge(ident_ready, 1)
                        pool.wait_ge(ld_par, 16)
                        for e in range(EH):
                            nc.gpsimd.tensor_tensor(diag_d[:, e, :], ident[:],
                                                    par_sb[:, e, C_D:C_D + 1].to_broadcast([P, P]),
                                                    ALU.mult).then_inc(diag_d_ready, 1)
                    elif what == "rstd":
                        pool.wait_ge(ve_done, 1)
                        pool.wait_ge(const_ready, 2)
                        nc.gpsimd.tensor_tensor(ln_rstd[:], ln_ve[:], minus_half[:],
                                                ALU.pow).then_inc(rstd_done, 1)
                    elif what == "rstd2":
                        c = slice(KD * b, KD * b + KD)
                        pool.wait_ge(ve2_done, b + 1)
                        nc.gpsimd.tensor_tensor(rstd2[:, c], ve2[:, c], minus_half[:, c],
                                                ALU.pow).then_inc(rstd2_done, 1)

            own_steps([("diag_d", 0, 0)])
            for s in range(len(after)):
                own_steps(before[s])
                if s < NT:
                    product(s)
                own_steps(middle[s])
                if s in HALVED:
                    halve(s)
                own_steps(after[s])

        @block.scalar
        def _(act):
            def conv_tanh(b):
                if b == 0:
                    act.wait_ge(half_conv_b_ready, 1)
                for e in range(EH):
                    act.wait_ge(conv_done, EH * b + (e if b == 0 else EH - 1) + 1)
                    bank = conv_bank(b, e)[:, e * L:(e + 1) * L]
                    nc.scalar.activation(conv[:, b, e, :], bank, ACT.Identity, bias=half_conv_b[:, e, :])
                    nc.scalar.activation(bank, bank, ACT.Tanh, bias=half_conv_b[:, e, :]).then_inc(conv_tanh_done, 1)

            def split_rows(b):
                act.wait_ge(rows_done, b + 1)
                if b >= 2:
                    act.wait_ge(dt_done, b - 1)
                nc.scalar.activation(dt_low[DT0:DT0 + DR, b % 2, :], ps_w1[DT0:DT0 + DR, 0:L],
                                     ACT.Copy).then_inc(dt_low_done, 1)
                if b >= 2:
                    act.wait_ge(c_stored, 16 * (b - 1))
                nc.scalar.activation(bc_rows[:, b % 2, :], ps_w1[0:BC, 0:L], ACT.Copy).then_inc(bc_rows_done, 1)
                nc.scalar.activation(bc_parts[:, b, :], ps_w1[0:3 * BC, 0:L],
                                     ACT.Copy).then_inc(bc_hi_done, 1)
                if b > 0:
                    act.wait_ge(c_stored, 16 * b)
                act.wait_ge(bc_rows_done, b + 1)
                nc.scalar.dma_start(c_rows[b], bc_rows[DS:BC, b % 2, :]).then_inc(c_stored, 16)

            def abs_dt(b):
                act.wait_ge(dt_done, b + 1)
                for e in range(EH):
                    nc.scalar.activation(dt_abs[:, b, e, :], ps_w0[:, e * L:(e + 1) * L], ACT.Abs,
                                         bias=par_sb[:, e, C_DTB:C_DTB + 1]).then_inc(dt_abs_done, 1)

            def relu_dt(b):
                for e in range(EH):
                    nc.scalar.activation(dt_x[:, b, e, :], ps_w0[:, e * L:(e + 1) * L], ACT.Relu,
                                         bias=par_sb[:, e, C_DTB:C_DTB + 1]).then_inc(dt_relu_done, 1)

            def softplus_log(bs):
                cuts = [(0, e, e + 1) for e in range(EH)] if bs == range(1) else [(b, 0, EH) for b in bs]
                for i, (b, e0, e1) in enumerate(cuts):
                    act.wait_ge(dt_abs_done, EH * b + e1)
                    nc.scalar.activation(dt_abs[:, b, e0:e1], dt_abs[:, b, e0:e1], ACT.Exp,
                                         scale=-1.0).then_inc(dt_exp_done, e1 - e0)
                for b, e0, e1 in cuts:
                    act.wait_ge(dt_exp_done, EH * b + e1)
                    nc.scalar.activation(dt_ln[:, b, e0:e1], dt_abs[:, b, e0:e1], ACT.Ln,
                                         bias=1.0).then_inc(dt_ln_done, e1 - e0)

            def decays(t):
                b, g, e = t // TPB, (t % TPB) // EH, t % EH
                if t == 0:
                    act.wait_ge(a_ready, 1)
                    act.wait_ge(decay_zeroed, N_DECAY)
                if t == 0 or t % TPB == 0 and b > 0:
                    act.wait_ge(delta_done, EH * b + (1 if b == 0 else EH))
                elif t == 1:
                    act.wait_ge(delta_done, EH)
                if t >= N_DECAY:
                    act.wait_ge(scan_done, 2 * (t - N_DECAY + 1))
                for n in range(NG):
                    last = nc.scalar.activation(decay[t % N_DECAY][:, n, 1:L], delta[:, b, e, 1:L], ACT.Exp,
                                                scale=a_neg[:, e, NG * g + n:NG * g + n + 1])
                    if n % 2 == 1:
                        last.then_inc(decay_done, 1)

            def own_steps(steps):
                for what, b, h in steps:
                    if what == "conv_tanh":
                        conv_tanh(b)
                    elif what == "split_rows":
                        split_rows(b)
                    elif what == "abs_dt":
                        abs_dt(b)
                    elif what == "relu_dt":
                        relu_dt(b)
                    elif what == "mid_rows":
                        act.wait_ge(bc_rest_done, b + 1)
                        nc.scalar.activation(bc_mid[2 * BC:3 * BC, b, :], bc_rest[2 * BC:3 * BC, b % 2, :],
                                             ACT.Copy).then_inc(bc_mid_done, 1)
                        nc.scalar.activation(bc_parts[BC:2 * BC, b, :], bc_rest[BC:2 * BC, b % 2, :],
                                             ACT.Copy).then_inc(bc_mid_done, 1)
                    elif what == "softplus_log":
                        softplus_log(range(1, NB))
                    elif what == "abs_w":
                        if b > 0:
                            act.wait_ge(abs_done, b)
                        if b < 2:
                            act.wait_ge((ld_w1, ld_w2)[b], 16)
                            nc.scalar.activation(w_below[:, 0:KD * H], w_up_in[:, b], ACT.Abs,
                                                 accum_out=abs_sum[:, b:b + 1]).then_inc(abs_done, 1)
                        else:
                            act.wait_ge(ld_w3, 16)
                            nc.scalar.activation(w_below[:, 0:HF * L], w_down_in[:, 0:HF, :], ACT.Abs,
                                                 accum_out=abs_sum[:, 2:3]).then_inc(abs_done, 1)
                            act.wait_ge(ld_w3l, 16)
                            act.wait_ge(abs_zeroed, 1)
                            act.wait_ge(abs_done, 3)
                            nc.scalar.activation(w_below[0:HL, 0:L], w_down_in[0:HL, HF, :], ACT.Abs,
                                                 accum_out=abs_sum[0:HL, 3:4]).then_inc(abs_done, 1)
                    elif what == "z_half":
                        if b == 0:
                            act.wait_ge(ln_half_done, 2)
                        act.wait_ge(delta_done, EH * (b + 1))
                        for e in range(EH):
                            c = KD * b + e
                            nc.scalar.activation(z_half[:, b, e, :], x_sb[:, b, e, :], ACT.Identity,
                                                 bias=ln_shift[:, c:c + 1],
                                                 scale=ln_half[:, c:c + 1]).then_inc(z_half_done, 1)
                    elif what == "z_tanh":
                        act.wait_ge(z_half_done, EH * (b + 1))
                        if b > 0:
                            act.wait_ge(gate_done, b)
                        nc.scalar.activation(z_tanh[:], z_half[:, b], ACT.Tanh).then_inc(z_tanh_done, 1)
                    elif what == "z2_hi":
                        act.wait_ge(z2_t_done, b + 1)
                        if b > 0:
                            act.wait_ge(up_done, HC * b)
                        nc.scalar.activation(z2_hi[:], ps_t[:].rearrange("p (k l) -> p k l", k=KD),
                                             ACT.Copy).then_inc(hi_done, 1)
                    elif what == "z2_mid":
                        act.wait_ge(rest_done, b + 1)
                        nc.scalar.activation(z2_mid[:], z2_rest[:], ACT.Copy).then_inc(mid_done, 1)
                    elif what == "up_tanh":
                        k = HC * b + h
                        rows = P if h < HF else HL
                        act.wait_ge(up_done, k + 1)
                        if k >= 2:
                            act.wait_ge(hidden_done, k - 1)
                        nc.scalar.activation(up_tanh[0:rows, k % 2, :], up_bank(h)[0:rows, 0:L], ACT.Tanh,
                                             scale=0.5).then_inc(up_tanh_done, 1)

            act.wait_ge(rows_ready, 1)
            nc.scalar.activation(pick[:, 0:DS], row_of3[:, 0:DS, None].to_broadcast([3 * BC, DS, P]),
                                 ACT.Copy).then_inc(pick_ready, 1)
            act.wait_ge(ld_par, 16)
            nc.scalar.activation(a_exp[:], par_sb[:, :, C_ALOG:C_ALOG + DS], ACT.Exp).then_inc(a_exp_ready, 1)
            conv_tanh(0)
            act.wait_ge(ld_g, 16)
            nc.scalar.activation(tanh_g[:], gains_sb[:], ACT.Tanh).then_inc(tanh_g_ready, 1)
            nc.scalar.preload_act_table_set("natural_log_exp_and_others")
            split_rows(0)
            abs_dt(0)
            softplus_log(range(1))
            decays(0)
            for s in range(len(after)):
                own_steps(before[s])
                if s + 1 < NT:
                    decays(s + 1)
                own_steps(middle[s])
                own_steps(after[s])

        @block.vector
        def _(dve):
            def silu_conv(b):
                for e in range(EH):
                    dve.wait_ge(conv_tanh_done, EH * b + (e if b == 0 else EH - 1) + 1)
                    nc.vector.scalar_tensor_tensor(out=u_sb[:, b, e, :],
                                                   in0=conv_bank(b, e)[:, e * L:(e + 1) * L], scalar=1.0,
                                                   in1=conv[:, b, e, :], op0=ALU.add,
                                                   op1=ALU.mult).then_inc(u_done, 1)

            def rest_rows(b):
                dve.wait_ge(bc_hi_done, b + 1)
                nc.vector.tensor_tensor(bc_rest[:, b % 2, :], ps_w1[0:3 * BC, 0:L], bc_parts[:, b, :],
                                        ALU.subtract).then_inc(bc_rest_done, 1)

            def low_rows(b):
                dve.wait_ge(bc_mid_done, 2 * b + 1)
                low = slice(2 * BC, 3 * BC)
                nc.vector.tensor_tensor(bc_parts[low, b, :], bc_rest[low, b % 2, :], bc_mid[low, b, :],
                                        ALU.subtract).then_inc(bc_lo_done, 1)

            def relu_dt():
                dve.wait_ge(dt_abs_done, EH)
                for e in range(EH):
                    nc.vector.tensor_scalar(dt_x[:, 0, e, :], ps_w0[:, e * L:(e + 1) * L],
                                            par_sb[:, e, C_DTB:C_DTB + 1], 0.0, ALU.add,
                                            ALU.max).then_inc(dt_relu_done, 1)

            def first_delta(e):
                dve.wait_ge(dt_ln_done, e + 1)
                dve.wait_ge(dt_relu_done, e + 1)
                nc.vector.tensor_tensor(delta[:, 0, e], dt_x[:, 0, e], dt_ln[:, 0, e],
                                        ALU.add).then_inc(delta_done, 1)
                dve.wait_ge(delta_done, e + 1)
                nc.vector.tensor_tensor(du[:, 0, e], delta[:, 0, e], u_sb[:, 0, e], ALU.mult).then_inc(du_done, 1)

            def scan_tile(t, between):
                b, g, e = t // TPB, (t % TPB) // EH, t % EH
                grp = t // EH
                if t % TPB == 0:
                    dve.wait_ge(du_done, EH * b + (1 if b == 0 else EH))
                elif t == 1:
                    dve.wait_ge(du_done, EH)
                if e == 0:
                    dve.wait_ge(b_rep_done, grp + 1)
                for q in range(2):
                    if t >= 1:
                        dve.wait_ge(scan_done, 2 * (t - 1) + q + 1)
                    nc.vector.tensor_tensor(
                        ps_db[:, q * QW:(q + 1) * QW].rearrange("p (n l) -> p n l", n=2),
                        du[:, b, e, None, :].to_broadcast([P, 2, L]),
                        ps_b[:, q * QW:(q + 1) * QW].rearrange("p (n l) -> p n l", n=2),
                        ALU.mult).then_inc(db_done, 1)
                own_steps(between)
                if t == 0:
                    first_delta(1)
                if t >= N_STATE:
                    dve.wait_ge(prod_done, t - N_STATE + 1)
                for q in range(2):
                    dve.wait_ge(decay_done, 2 * t + q + 1)
                    dve.wait_ge(db_done, 2 * t + q + 1)
                    nc.vector.tensor_tensor_scan(
                        state[t % N_STATE][:].rearrange("p n l -> p (n l)")[:, q * QW:(q + 1) * QW],
                        decay[t % N_DECAY][:].rearrange("p n l -> p (n l)")[:, q * QW:(q + 1) * QW],
                        ps_db[:, q * QW:(q + 1) * QW], 0.0, ALU.mult, ALU.add).then_inc(scan_done, 1)

            def last_product():
                t = NT - 1
                dve.wait_ge(scan_done, 2 * NT)
                dve.wait_ge(c_loaded[(t // EH) % N_CREP], 16 * (t // EH // N_CREP + 1))
                dve.wait_ge(sum_done, t - N_PROD + 1)
                nc.vector.tensor_tensor(prod[t % N_PROD][:, NG // 2:NG], state[t % N_STATE][:, NG // 2:NG],
                                        c_rep[(t // EH) % N_CREP][:, NG // 2:NG], ALU.mult).then_inc(last_prod_done, 1)

            nc.vector.memset(zeros[:], 0.0).then_inc(zeros_ready, 1)
            dve.wait_ge(ld_win, 16)
            for e in range(EH):
                dve.wait_ge((ld_conv, ld_conv1)[e], 16)
                cs = slice(e * P, (e + 1) * P)
                nc.vector.scalar_tensor_tensor(
                    out=win_tap[:, :, cs], in0=conv_rep[:, :, cs], scalar=0.5,
                    in1=win_sb[:, None, cs].to_broadcast([P, DC, P]), op0=ALU.mult,
                    op1=ALU.mult).then_inc(win_tap_ready, 1)
            dve.wait_ge(ld_par, 16)
            nc.vector.tensor_scalar(half_conv_b[:], par_sb[:, :, C_CONVB:C_CONVB + 1], 0.5, None,
                                    ALU.mult).then_inc(half_conv_b_ready, 1)
            dve.wait_ge(ld_xw, 16)
            for k in range(3):
                nc.vector.tensor_copy(xw_sb[:, :, k * BC:(k + 1) * BC], xw_in[:, :, 0:BC]).then_inc(xw_ready, 1)
            nc.vector.tensor_copy(xw_sb[:, :, DT0:DT0 + DR], xw_in[:, :, BC:BC + DR]).then_inc(xw_ready, 1)
            for i in range(N_DECAY):
                nc.vector.memset(decay[i][:, :, 0:1], 0.0).then_inc(decay_zeroed, 1)
            def own_steps(steps):
                for what, b, h in steps:
                    if what == "silu_conv":
                        silu_conv(b)
                    elif what == "rest_rows":
                        if b >= 2:
                            dve.wait_ge(bc_lo_done, b - 1)
                            dve.wait_ge(bc_mid_done, 2 * (b - 1))
                        rest_rows(b)
                    elif what == "low_rows":
                        low_rows(b)
                    elif what == "stats":
                        dve.wait_ge(ld_x, 16)
                        cs = range(b * NB * KD // 2, (b + 1) * NB * KD // 2)
                        for c in cs:
                            nc.vector.bn_stats(ln_stats[:, c, :], x_sb[:, c // KD, c % KD, :]).then_inc(stats_done, 1)
                        for c in cs:
                            dve.wait_ge(stats_done, c + 1)
                            nc.vector.bn_aggr(ln_mv[:, c, :], ln_stats[:, c, :]).then_inc(mv_done, 1)
                        if b == 1:
                            dve.wait_ge(mv_done, NB * KD)
                            nc.vector.tensor_scalar(ln_ve[:], ln_mv[:, :, 1], LN_EPS, None,
                                                    ALU.add).then_inc(ve_done, 1)
                    elif what == "ln_shift":
                        dve.wait_ge(rstd_done, 1)
                        nc.vector.tensor_scalar(ln_half[:], ln_rstd[:], 0.5, None,
                                                ALU.mult).then_inc(ln_half_done, 1)
                        dve.wait_ge(ln_half_done, 1)
                        nc.vector.scalar_tensor_tensor(out=ln_shift[:], in0=ln_mv[:, :, 0], scalar=-1.0,
                                                       in1=ln_half[:], op0=ALU.mult,
                                                       op1=ALU.mult).then_inc(ln_half_done, 1)
                    elif what == "thresholds":
                        dve.wait_ge(gamma_done, 1)
                        nc.vector.tensor_scalar(thr[:, 0:2], ps_w1[:, 0:2], 0.5 / (H * L), 0.5 * Q_EPS,
                                                ALU.mult, ALU.add).then_inc(thr_step, 1)
                        nc.vector.tensor_reduce(thr[:, 3:4], ps_w1[:, 2:4], AX_X, ALU.add).then_inc(thr_step, 1)
                        dve.wait_ge(thr_step, 2)
                        nc.vector.tensor_scalar(thr[:, 2:3], thr[:, 3:4], 0.5 / (H * L), 0.5 * Q_EPS,
                                                ALU.mult, ALU.add).then_inc(thr_step, 1)
                        dve.wait_ge(thr_step, 3)
                        nc.vector.tensor_scalar(thr_neg[:, 0:3], thr[:, 0:3], -1.0, None,
                                                ALU.mult).then_inc(thr_step, 1)
                    elif what == "quant" and b < 2:
                        dve.wait_ge(thr_step, 4)
                        if b > 0:
                            dve.wait_ge(quant_done, 2 * b)
                        below = w_below[:, 0:KD * H].rearrange("p (k h) -> p k h", k=KD)
                        nc.vector.tensor_scalar(below, w_up_in[:, b], thr_neg[:, b:b + 1], None,
                                                ALU.is_lt).then_inc(below_done, 1)
                        dve.wait_ge(below_done, b + 1)
                        full, rest = HF * P, 2 * HF * P + b * HL
                        for src, dst in ((slice(0, full), slice(b * full, (b + 1) * full)),
                                         (slice(full, H), slice(rest, rest + HL))):
                            nc.vector.scalar_tensor_tensor(
                                out=w_up_q[:, :, dst], in0=w_up_in[:, b, :, src], scalar=thr[:, b:b + 1],
                                in1=below[:, :, src], op0=ALU.is_gt, op1=ALU.subtract).then_inc(quant_done, 1)
                    elif what == "quant":
                        dve.wait_ge(quant_done, 4)
                        below = w_below[:, 0:HC * L].rearrange("p (c d) -> p c d", c=HC)
                        for rows, cs in ((P, slice(0, HF)), (HL, slice(HF, HC))):
                            nc.vector.tensor_scalar(below[0:rows, cs], w_down_in[0:rows, cs], thr_neg[0:rows, 2:3],
                                                    None, ALU.is_lt).then_inc(below_done, 1)
                        dve.wait_ge(below_done, 4)
                        for rows, cs in ((P, slice(0, HF)), (HL, slice(HF, HC))):
                            nc.vector.scalar_tensor_tensor(
                                out=w_down_q[0:rows, cs], in0=w_down_in[0:rows, cs], scalar=thr[0:rows, 2:3],
                                in1=below[0:rows, cs], op0=ALU.is_gt, op1=ALU.subtract).then_inc(quant_done, 1)
                    elif what == "half_gain":
                        dve.wait_ge(tanh_g_ready, 1)
                        nc.vector.tensor_scalar(half_tanh_g[:], tanh_g[:], 0.5, None,
                                                ALU.mult).then_inc(half_g_ready, 1)
                    elif what == "gate":
                        dve.wait_ge(z_tanh_done, b + 1)
                        dve.wait_ge(delta_done, EH * (b + 1))
                        nc.vector.scalar_tensor_tensor(out=gate[:, b], in0=z_tanh[:], scalar=1.0, in1=z_half[:, b],
                                                       op0=ALU.add, op1=ALU.mult).then_inc(gate_done, 1)
                    elif what == "mix":
                        dve.wait_ge(sum_done, TPB * (b + 1))
                        dve.wait_ge(gate_done, b + 1)
                        if b > 0:
                            dve.wait_ge(mixed_t_done, b)
                        nc.vector.scalar_tensor_tensor(
                            out=mixed[:], in0=ps_y[:].rearrange("p (e l) -> p e l", e=EH),
                            scalar=tanh_g[:, 0:1], in1=gate[:, b], op0=ALU.mult, op1=ALU.mult).then_inc(mixed_done, 1)
                    elif what == "x1":
                        dve.wait_ge(mixed_t_done, b + 1)
                        if b >= 2:
                            dve.wait_ge(out_done, KD * (b - 1))
                        nc.vector.tensor_tensor(x1_sb[:, b % 2], x_sb[:, b],
                                                ps_t[:].rearrange("p (t l) -> p t l", t=KD),
                                                ALU.add).then_inc(x1_done, 1)
                        dve.wait_ge(x1_done, b + 1)
                        for t in range(KD):
                            nc.vector.bn_stats(st2[:, KD * b + t, :], x1_sb[:, b % 2, t, :]).then_inc(st2_done, 1)
                        for t in range(KD):
                            dve.wait_ge(st2_done, KD * b + t + 1)
                            nc.vector.bn_aggr(mv2[:, KD * b + t, :], st2[:, KD * b + t, :]).then_inc(mv2_done, 1)
                        dve.wait_ge(mv2_done, KD * (b + 1))
                        c = slice(KD * b, KD * b + KD)
                        nc.vector.tensor_scalar(ve2[:, c], mv2[:, c, 1], LN_EPS, None, ALU.add).then_inc(ve2_done, 1)
                    elif what == "z2_lo":
                        dve.wait_ge(mid_done, b + 1)
                        if b > 0:
                            dve.wait_ge(up_done, HC * b)
                        nc.vector.tensor_tensor(z2_lo[:], z2_rest[:], z2_mid[:],
                                                ALU.subtract).then_inc(lo_done, 1)
                    elif what == "shift2":
                        c = slice(KD * b, KD * b + KD)
                        dve.wait_ge(rstd2_done, b + 1)
                        nc.vector.scalar_tensor_tensor(out=shift2[:, c], in0=mv2[:, c, 0], scalar=-1.0,
                                                       in1=rstd2[:, c], op0=ALU.mult,
                                                       op1=ALU.mult).then_inc(shift2_done, 1)
                    elif what == "z2":
                        dve.wait_ge(shift2_done, b + 1)
                        if b > 0:
                            dve.wait_ge(z2_t_done, b)
                        for t in range(KD):
                            c = KD * b + t
                            nc.vector.tensor_scalar(z2_sb[:, t, :], x1_sb[:, b % 2, t, :], rstd2[:, c:c + 1],
                                                    shift2[:, c:c + 1], ALU.mult, ALU.add).then_inc(z2_done, 1)
                    elif what == "z2_rest":
                        dve.wait_ge(hi_done, b + 1)
                        nc.vector.tensor_tensor(z2_rest[:], ps_t[:].rearrange("p (k l) -> p k l", k=KD),
                                                z2_hi[:], ALU.subtract).then_inc(rest_done, 1)
                    elif what == "hidden":
                        k = HC * b + h
                        rows = P if h < HF else HL
                        dve.wait_ge(up_tanh_done, k + 1)
                        if b >= 2 and h == 0:
                            dve.wait_ge(down_done, b - 1)
                        x2 = up_bank(h)[:, L:2 * L] if h < HF else up_bank(h)[HL:2 * HL, 0:L]
                        nc.vector.scalar_tensor_tensor(out=hidden[0:rows, b % 2, h, :],
                                                       in0=up_tanh[0:rows, k % 2, :], scalar=1.0, in1=x2,
                                                       op0=ALU.add, op1=ALU.mult).then_inc(hidden_done, 1)
                    elif what == "out":
                        dve.wait_ge(down_done, b + 1)
                        for t in range(KD):
                            nc.vector.scalar_tensor_tensor(
                                out=x_sb[:, b, t, :], in0=ps_w1[:, t * L:(t + 1) * L],
                                scalar=half_tanh_g[:, 1:2], in1=x1_sb[:, b % 2, t, :],
                                op0=ALU.mult, op1=ALU.add).then_inc(out_done, 1)

            dve.wait_ge(a_exp_ready, 1)
            nc.vector.tensor_scalar(a_neg[:], a_exp[:], -1.0, None, ALU.mult).then_inc(a_ready, 1)
            silu_conv(0)
            rest_rows(0)
            dve.wait_ge(bc_rest_done, 1)
            nc.vector.tensor_copy(bc_mid[2 * BC:3 * BC, 0, :], bc_rest[2 * BC:3 * BC, 0, :]).then_inc(bc_mid_done, 1)
            nc.vector.tensor_copy(bc_parts[BC:2 * BC, 0, :], bc_rest[BC:2 * BC, 0, :]).then_inc(bc_mid_done, 1)
            low_rows(0)
            relu_dt()
            first_delta(0)
            for s in range(len(after)):
                if s == 1:
                    own_steps([("half_gain", 0, 0)])
                own_steps(before[s])
                if s < NT:
                    scan_tile(s, middle[s])
                    if s == NT - 1:
                        last_product()
                else:
                    own_steps(middle[s])
                own_steps(after[s])

        @block.tensor
        def _(pe):
            issued = {step: 0 for step in ("conv", "rows", "dt", "gamma", "mix_t", "z2_t", "up")}

            def convolve(b):
                if b < 2:
                    pe.wait_ge(ld_ctx0 if b == 0 else ld_ctx, 16)
                if b == 2:
                    pe.wait_ge(dt_relu_done, EH * issued["dt"])
                elif b == 3:
                    pe.wait_ge(bc_rest_done, issued["rows"])
                    if issued["gamma"] > 0:
                        pe.wait_ge(thr_step, 2)
                issued["conv"] += 1
                for e in range(EH):
                    if b == 0:
                        pe.wait_ge(win_tap_ready, e + 1)
                    for k in range(DC):
                        last = nc.tensor.matmul(conv_bank(b, e)[:, e * L + k:(e + 1) * L],
                                                win_tap[:, DC - 1 - k, e * P:(e + 1) * P],
                                                ctx_sb[:, b, 0:L - k], start=(k == 0), stop=(k == DC - 1),
                                                skip_group_check=True)
                    last.then_inc(conv_done, 1)

            def rows_bc_dt(b):
                if b == 0:
                    pe.wait_ge(xw_ready, 4)
                if b > 0:
                    pe.wait_ge(bc_rest_done, b)
                if issued["gamma"] > 0:
                    pe.wait_ge(thr_step, 2)
                if issued["conv"] == NB:
                    pe.wait_ge(u_done, EH * NB)
                issued["rows"] += 1
                for e in range(EH):
                    pe.wait_ge(u_done, EH * b + (e if b == 0 else EH - 1) + 1)
                    last = nc.tensor.matmul(ps_w1[0:DT0 + DR, 0:L], xw_sb[:, e, :], u_sb[:, b, e, :],
                                            start=(e == 0), stop=(e == EH - 1))
                last.then_inc(rows_done, 1)

            def project_dt(b):
                if b == 0:
                    pe.wait_ge(ld_dtw, 16)
                if b > 0:
                    pe.wait_ge(dt_relu_done, EH * b)
                if issued["conv"] >= 3:
                    pe.wait_ge(u_done, EH * 3)
                issued["dt"] += 1
                pe.wait_ge(dt_low_done, b + 1)
                for e in range(EH):
                    last = nc.tensor.matmul(ps_w0[:, e * L:(e + 1) * L],
                                            dtw_sb[DT0:DT0 + DR, e * P:(e + 1) * P],
                                            dt_low[DT0:DT0 + DR, b % 2, :], start=True, stop=True)
                last.then_inc(dt_done, 1)

            def spread_b(grp):
                b, g = grp // NGRP, grp % NGRP
                if g == 0:
                    pe.wait_ge(bc_mid_done, 2 * (b + 1))
                    pe.wait_ge(bc_lo_done, b + 1)
                if grp == 0:
                    pe.wait_ge(pick_ready, 1)
                else:
                    pe.wait_ge(db_done, 2 * EH * grp)
                for n in range(NG):
                    last = nc.tensor.matmul(ps_b[:, n * L:(n + 1) * L], pick[:, NG * g + n, :],
                                            bc_parts[:, b, :], start=True, stop=True)
                last.then_inc(b_rep_done, 1)

            def sum_states(t):
                b, g, e = t // TPB, (t % TPB) // EH, t % EH
                if t in HALVED:
                    pe.wait_ge(prod_half_done, HALVED.index(t) + 1)
                else:
                    pe.wait_ge(prod_done, t + 1)
                if t == NT - 1:
                    pe.wait_ge(last_prod_done, 1)
                left = NG // 2 if t in HALVED else NG
                if t % TPB == 0:
                    if b == 0:
                        pe.wait_ge(u_done, EH * 2)
                    else:
                        pe.wait_ge(mixed_done, b)
                    if b == 0:
                        pe.wait_ge(diag_d_ready, EH)
                    for half in range(EH):
                        nc.tensor.matmul(ps_y[:, half * L:(half + 1) * L], diag_d[:, half, :], u_sb[:, b, half, :],
                                         start=(half == 0), stop=False, skip_group_check=True)
                for n in range(left):
                    last = nc.tensor.matmul(ps_y[:, e * L:(e + 1) * L], ident[:], prod[t % N_PROD][:, n, :],
                                            start=False,
                                            stop=(t % TPB == TPB - 1 and n == left - 1), skip_group_check=True)
                last.then_inc(sum_done, 1)

            def own_steps(steps):
                for what, b, h in steps:
                    if what == "conv":
                        convolve(b)
                    elif what == "rows":
                        rows_bc_dt(b)
                    elif what == "dt":
                        project_dt(b)
                    elif what == "gamma":
                        pe.wait_ge(abs_done, 4)
                        pe.wait_ge(const_ready, 2)
                        pe.wait_ge(bc_rest_done, issued["rows"])
                        if issued["conv"] == NB:
                            pe.wait_ge(u_done, EH * NB)
                        issued["gamma"] += 1
                        nc.tensor.matmul(ps_w1[:, 0:4], ones[:], abs_sum[:], start=True,
                                         stop=True).then_inc(gamma_done, 1)
                    elif what == "mix_t":
                        pe.wait_ge(mixed_done, b + 1)
                        if b > 0:
                            pe.wait_ge(rest_done, b)
                        if issued["up"] > 0:
                            pe.wait_ge(hidden_done, issued["up"])
                        issued["mix_t"] += 1
                        for t in range(KD):
                            for e in range(EH):
                                last = nc.tensor.transpose(ps_t[:, t * L + e * P:t * L + (e + 1) * P],
                                                           mixed[:, e, t * P:(t + 1) * P], ident[:])
                        last.then_inc(mixed_t_done, 1)
                    elif what == "z2_t":
                        pe.wait_ge(z2_done, KD * (b + 1))
                        pe.wait_ge(x1_done, b + 1)
                        if issued["up"] > 0:
                            pe.wait_ge(hidden_done, issued["up"])
                        issued["z2_t"] += 1
                        for k in range(KD):
                            for t in range(KD):
                                last = nc.tensor.transpose(ps_t[:, k * L + t * P:k * L + (t + 1) * P],
                                                           z2_sb[:, t, k * P:(k + 1) * P], ident[:])
                        last.then_inc(z2_t_done, 1)
                    elif what == "up":
                        k = HC * b + h
                        if h == 0 and b == 0:
                            pe.wait_ge(quant_done, 4)
                        if k == 0:
                            pe.wait_ge(dt_relu_done, EH * NB)
                        elif h % 2:
                            pe.wait_ge(x1_done, issued["mix_t"])
                            pe.wait_ge(rest_done, issued["z2_t"])
                        if k >= 2:
                            pe.wait_ge(hidden_done, k - 1)
                        issued["up"] += 1
                        bank = up_bank(h)
                        if h < HF:
                            cols = ((h * P, slice(0, L)), ((HF + h) * P, slice(L, 2 * L)))
                        else:
                            cols = ((2 * HF * P, slice(0, L)),)
                        for i, (z, split_done) in enumerate(((z2_hi, hi_done), (z2_mid, mid_done), (z2_lo, lo_done))):
                            if h == 0:
                                pe.wait_ge(split_done, b + 1)
                            for j, (at, where) in enumerate(cols):
                                for kd in range(KD):
                                    last = nc.tensor.matmul(bank[:, where], w_up_q[:, kd, at:at + P], z[:, kd, :],
                                                            start=(i == 0 and j == 0 and kd == 0),
                                                            stop=(i == 2 and j == len(cols) - 1 and kd == KD - 1),
                                                            skip_group_check=True)
                        last.then_inc(up_done, 1)
                    elif what == "down":
                        rows = P if h < HF else HL
                        pe.wait_ge(hidden_done, HC * b + h + 1)
                        if h == 0:
                            if b == 0:
                                pe.wait_ge(quant_done, 6)
                                pe.wait_ge(bc_rest_done, NB)
                                pe.wait_ge(thr_step, 2)
                            else:
                                pe.wait_ge(out_done, KD * b)
                        for t in range(KD):
                            last = nc.tensor.matmul(ps_w1[:, t * L:(t + 1) * L],
                                                    hidden[0:rows, b % 2, h, t * P:(t + 1) * P],
                                                    w_down_q[0:rows, h, :], start=(h == 0 and t == 0),
                                                    stop=(h == HC - 1 and t == KD - 1), skip_group_check=True)
                        if h == HC - 1:
                            last.then_inc(down_done, 1)

            pe.wait_ge(zeros_ready, 1)
            for i in range(N_WARM):
                nc.tensor.matmul(ps_w1[:], zeros[:, 0:P], zeros[:], start=True, stop=True)
            convolve(0)
            rows_bc_dt(0)
            project_dt(0)
            spread_b(0)
            for s in range(len(after)):
                own_steps(before[s])
                if s == 0:
                    pe.wait_ge(ident_ready, 1)
                if LAG <= s < NT:
                    sum_states(s - LAG)
                if s == NT:
                    for t in range(NT - LAG, NT):
                        sum_states(t)
                own_steps(middle[s])
                if s % 2 == 1 and s + 1 < NT:
                    spread_b((s + 1) // 2)
                own_steps(after[s])


def kernel(**inputs):
    import numpy as np
    import concourse.bacc as bacc
    from concourse.bass_utils import run_bass_kernel_spmd

    a = {k: np.asarray(v) for k, v in inputs.items()}
    pre = "L0_xattn_"
    xw = a[pre + "x_proj_w"]
    arrays = {
        "x": a["x"],
        "ctxT": a["ctx_1024"].transpose(2, 0, 1),
        "gains": np.concatenate([a["g_xattn"], a["g_ffn"]]),
        "winT": a[pre + "in_proj_w"].T,
        "convT": a[pre + "conv_w"].T,
        "par": np.concatenate([a[pre + "conv_b"][:, None], a[pre + "dt_proj_b"][:, None], a[pre + "A_log"],
                               a[pre + "D"][:, None]], axis=1),
        "xwT": np.concatenate([xw[DR:], xw[:DR]], axis=0).T,
        "dtwT": a[pre + "dt_proj_w"].T,
        "w1T": a["L0_ffn_w1"].T,
        "w2T": a["L0_ffn_w2"].T,
        "w3T": a["L0_ffn_w3"].T,
    }
    nc = bacc.Bacc("TRN2", target_bir_lowering=False, num_devices=1)
    ins, args = {}, []
    for name, v in arrays.items():
        v = np.ascontiguousarray(v)
        ins[f"in_{name}"] = v
        args.append(nc.dram_tensor(f"in_{name}", v.shape, mybir.dt.from_np(v.dtype), kind="ExternalInput").ap())
    c_rows = nc.dram_tensor("c_rows", (NB, DS, L), F32, kind="Internal").ap()
    out = nc.dram_tensor("out_0", (NB, L, L), F32, kind="ExternalOutput").ap()
    gated_ssm_ffn_kernel(nc, *args, c_rows, out)
    r = run_bass_kernel_spmd(nc, [ins], core_ids=[0])
    return r.results[0]["out_0"]
```

```python
from contextlib import ExitStack

import concourse.bass as bass
from concourse import mybir

F32 = mybir.dt.float32
BF16 = mybir.dt.bfloat16
ALU = mybir.AluOpType
ACT = mybir.ActivationFunctionType
AX_X = mybir.AxisListType.X

P = 128
NB = 4
L = 256
DM = 128
DI = 256
EH = DI // P
DS = 16
DR = 8
DC = 4
H = 704
HC = 6
HF = H // P
HL = H - HF * P
KD = L // P
NG = 4
NGRP = DS // NG
TPB = NGRP * EH
NT = NB * TPB
QW = 512
LN_EPS = 1e-5
Q_EPS = 1e-8

N_DECAY = 3
N_STATE = 4
N_PROD = 4
N_CREP = 3
N_WARM = 8
LAG = 2

HALVED = [0, 2, 4, 6, 7, 8, 12, 14, 17, 19, 21, 22, 24, 25, 26, 27, 28]

BEFORE, MIDDLE, AFTER = range(3)

C_ALOG, C_D = 0, DS
NPAR = C_D + 1
BC = 2 * DS
DT0 = 3 * BC


PLAN = [
    (0, AFTER, [("conv", 1, 0), ("rstd", 0, 0)]),
    (1, MIDDLE, [("abs_w", 0, 0), ("conv_tanh", 1, 0)]),
    (1, AFTER, [("conv", 2, 0), ("stats", 1, 0), ("silu_conv", 1, 0)]),
    (2, MIDDLE, [("ln_shift", 0, 0)]),
    (3, MIDDLE, [("z_half", 0, 0)]),
    (3, AFTER, [("rows", 1, 0), ("gate", 0, 0)]),
    (4, MIDDLE, [("dt", 1, 0), ("z_tanh", 0, 0), ("conv_tanh", 2, 0), ("silu_conv", 2, 0)]),
    (4, AFTER, [("rest_rows", 1, 0)]),
    (5, MIDDLE, [("split_rows", 1, 0), ("abs_w", 1, 0), ("abs_dt", 1, 0), ("mid_rows", 1, 0),
                 ("softplus_log", 1, 0), ("relu_dt", 1, 0)]),
    (5, AFTER, [("rows", 2, 0), ("low_rows", 1, 0)]),
    (6, MIDDLE, [("split_rows", 2, 0)]),
    (6, AFTER, [("softplus_sum", 1, 0)]),
    (7, BEFORE, [("delta_u", 1, 0)]),
    (7, MIDDLE, [("mid_rows", 2, 0), ("z_half", 1, 0), ("rest_rows", 2, 0)]),
    (7, AFTER, [("conv", 3, 0), ("low_rows", 2, 0)]),
    (8, BEFORE, [("z_tanh", 1, 0)]),
    (9, MIDDLE, [("gate", 1, 0), ("rstd2", 0, 0)]),
    (9, AFTER, [("dt", 2, 0), ("mix_t", 0, 0), ("mix", 0, 0)]),
    (10, MIDDLE, [("x1", 0, 0)]),
    (10, AFTER, [("abs_dt", 2, 0), ("shift2", 0, 0)]),
    (11, MIDDLE, [("z2_t", 0, 0), ("relu_dt", 2, 0), ("softplus_log", 2, 0), ("z2", 0, 0),
                  ("softplus_sum", 2, 0)]),
    (12, MIDDLE, [("z2_hi", 0, 0), ("z2_rest", 0, 0)]),
    (12, AFTER, [("z2_lo", 0, 0)]),
    (13, MIDDLE, [("z2_mid", 0, 0), ("conv_tanh", 3, 0), ("silu_conv", 3, 0), ("delta_u", 2, 0)]),
    (13, AFTER, [("rows", 3, 0)]),
    (14, MIDDLE, [("dt", 3, 0), ("gamma", 0, 0), ("z_half", 2, 0), ("split_rows", 3, 0), ("z_tanh", 2, 0),
                  ("abs_w", 2, 0), ("abs_dt", 3, 0), ("mid_rows", 3, 0), ("rest_rows", 3, 0)]),
    (15, BEFORE, [("softplus_log", 3, 0)]),
    (15, MIDDLE, [("thresholds", 0, 0), ("softplus_sum", 3, 0), ("delta_u", 3, 0)]),
    (15, AFTER, [("low_rows", 3, 0), ("quant", 0, 0)]),
    (16, MIDDLE, [("quant", 1, 0), ("rstd2", 1, 0)]),
    (16, AFTER, [("mix", 1, 0)]),
    (17, BEFORE, [("relu_dt", 3, 0)]),
    (17, MIDDLE, [("up", 0, 0), ("mix_t", 1, 0), ("x1", 1, 0)]),
    (17, AFTER, [("z_half", 3, 0), ("hidden", 0, 0), ("shift2", 1, 0)]),
    (18, MIDDLE, [("up", 0, 1), ("up", 0, 2), ("up", 0, 3), ("up_tanh", 0, 0), ("z2", 1, 0)]),
    (18, AFTER, [("hidden", 0, 1)]),
    (19, MIDDLE, [("up_tanh", 0, 1), ("quant", 2, 0), ("hidden", 0, 2)]),
    (19, AFTER, [("hidden", 0, 3)]),
    (20, MIDDLE, [("up", 0, 4), ("down", 0, 0), ("up", 0, 5), ("down", 0, 1), ("z2_t", 1, 0),
                  ("down", 0, 2), ("up_tanh", 0, 2), ("up_tanh", 0, 3), ("gate", 2, 0), ("hidden", 0, 4),
                  ("hidden", 0, 5)]),
    (21, BEFORE, [("up_tanh", 0, 4)]),
    (21, MIDDLE, [("down", 0, 3), ("up_tanh", 0, 5), ("z_tanh", 3, 0), ("z2_hi", 1, 0), ("z2_rest", 1, 0)]),
    (21, AFTER, [("z2_lo", 1, 0)]),
    (22, MIDDLE, [("up", 1, 0), ("down", 0, 4), ("up", 1, 1), ("z2_mid", 1, 0), ("gate", 3, 0)]),
    (23, BEFORE, [("up_tanh", 1, 0), ("hidden", 1, 0)]),
    (23, MIDDLE, [("down", 0, 5)]),
    (23, AFTER, [("up", 1, 2), ("out", 0, 0)]),
    (24, MIDDLE, [("up", 1, 3), ("up_tanh", 1, 1), ("hidden", 1, 1)]),
    (24, AFTER, [("hidden", 1, 2)]),
    (25, MIDDLE, [("up", 1, 4), ("up_tanh", 1, 2)]),
    (25, AFTER, [("mix", 2, 0), ("hidden", 1, 3)]),
    (26, BEFORE, [("up_tanh", 1, 3)]),
    (26, MIDDLE, [("mix_t", 2, 0), ("down", 1, 0), ("down", 1, 1), ("hidden", 1, 4), ("rstd2", 2, 0)]),
    (26, AFTER, [("down", 1, 2), ("x1", 2, 0)]),
    (27, MIDDLE, [("up", 1, 5), ("up_tanh", 1, 4)]),
    (27, AFTER, [("down", 1, 3), ("z2_t", 2, 0), ("shift2", 2, 0), ("hidden", 1, 5), ("z2", 2, 0)]),
    (28, MIDDLE, [("down", 1, 4), ("down", 1, 5), ("up_tanh", 1, 5), ("z2_rest", 2, 0)]),
    (28, AFTER, [("z2_lo", 2, 0)]),
    (29, MIDDLE, [("up", 2, 0), ("z2_hi", 2, 0), ("z2_mid", 2, 0), ("out", 1, 0)]),
    (29, AFTER, [("up", 2, 1)]),
    (30, MIDDLE, [("up", 2, 2), ("up_tanh", 2, 0), ("up_tanh", 2, 1), ("up_tanh", 2, 2), ("up_tanh", 2, 3),
                  ("up_tanh", 2, 4), ("up_tanh", 2, 5), ("z2_hi", 3, 0), ("z2_mid", 3, 0),
                  ("up_tanh", 3, 0), ("up_tanh", 3, 1), ("up_tanh", 3, 2), ("up_tanh", 3, 3),
                  ("up_tanh", 3, 4), ("up_tanh", 3, 5), ("hidden", 2, 0)]),
    (31, MIDDLE, [("up", 2, 3), ("hidden", 2, 1), ("hidden", 2, 2), ("rstd2", 3, 0)]),
    (31, AFTER, [("hidden", 2, 3), ("mix", 3, 0), ("x1", 3, 0), ("hidden", 2, 4), ("shift2", 3, 0),
                 ("z2", 3, 0), ("hidden", 2, 5), ("z2_rest", 3, 0), ("z2_lo", 3, 0), ("out", 2, 0),
                 ("hidden", 3, 0), ("hidden", 3, 1), ("hidden", 3, 2), ("hidden", 3, 3), ("hidden", 3, 4),
                 ("hidden", 3, 5), ("out", 3, 0)]),
    (32, AFTER, [("up", 2, 4), ("mix_t", 3, 0), ("down", 2, 0), ("down", 2, 1), ("up", 2, 5),
                 ("down", 2, 2), ("z2_t", 3, 0), ("down", 2, 3), ("down", 2, 4), ("down", 2, 5),
                 ("up", 3, 0), ("up", 3, 1), ("up", 3, 2), ("up", 3, 3), ("up", 3, 4), ("up", 3, 5)]),
    (33, AFTER, [("down", 3, 0), ("down", 3, 1), ("down", 3, 2), ("down", 3, 3), ("down", 3, 4),
                 ("down", 3, 5)]),
]


def schedule():
    lists = [[[] for _ in range(NT + 20)] for _ in range(3)]
    for slot, place, steps in PLAN:
        lists[place][slot] += steps
    return lists


def gated_ssm_ffn_kernel(nc, x, ctxT, gains, winT, convT, par, xwT, dtwT, w1T, w2T, w3T, c_rows, out):
    before, middle, after = schedule()
    with ExitStack() as es:
        def sb(name, shape, dt=F32):
            return es.enter_context(nc.sbuf_tensor(name, shape, dt))

        def psum(name, cols):
            return es.enter_context(nc.psum_tensor(name, [P, cols], F32))

        def sem(name):
            return es.enter_context(nc.semaphore(name))

        par_sb = sb("par_sb", [P, EH, NPAR])
        conv_b = sb("conv_b", [1, DI])
        half_conv_b = sb("half_conv_b", [1, DI])
        ones_row = sb("ones_row", [1, L])
        conv_rep = sb("conv_rep", [P, DC, DI])
        win_tap = sb("win_tap", [P, DC, DI])
        a_neg = sb("a_neg", [P, EH, DS])
        a_exp = sb("a_exp", [P, EH, DS])
        gains_sb = sb("gains_sb", [P, 2])
        tanh_g = sb("tanh_g", [P, 2])
        half_tanh_g = sb("half_tanh_g", [P, 2])
        win_sb = sb("win_sb", [P, DI])
        ctx_sb = sb("ctx_sb", [P, NB, L])
        xw_in = sb("xw_in", [P, EH, BC + DR])
        xw_sb = sb("xw_sb", [P, EH, DT0 + DR])
        dtw_sb = sb("dtw_sb", [P, DI])
        x_sb = sb("x_sb", [P, NB, KD, L])
        w_up_in = sb("w_up_in", [P, 2, KD, H])
        w_down_in = sb("w_down_in", [P, HC, L])
        w_below = sb("w_below", [P, HC * L], BF16)
        w_up_q = sb("w_up_q", [P, KD, 2 * H], BF16)
        w_down_q = sb("w_down_q", [P, HC, L])
        abs_sum = sb("abs_sum", [P, 4])
        thr = sb("thr", [P, 4])
        thr_neg = sb("thr_neg", [P, 4])
        ident = sb("ident", [P, P])
        diag_d = sb("diag_d", [P, EH, P])
        ones = sb("ones", [P, P])
        zeros = sb("zeros", [P, QW], BF16)
        row_of3 = sb("row_of3", [3 * BC, BC], BF16)
        pick = sb("pick", [3 * BC, DS, P], BF16)

        conv_th = sb("conv_th", [P, NB, EH, L])
        u_sb = sb("u_sb", [P, NB, EH, L])
        dt_low = sb("dt_low", [P, 2, L])
        bc_parts = sb("bc_parts", [3 * BC, NB, L], BF16)
        bc_rest = sb("bc_rest", [3 * BC, 2, L])
        bc_rows = sb("bc_rows", [BC, 2, L])
        bc_mid = sb("bc_mid", [3 * BC, NB, L], BF16)
        dt_x = sb("dt_x", [P, NB, EH, L])
        dt_abs = conv_th
        dt_ln = sb("dt_ln", [P, NB, EH, L])
        delta = sb("delta", [P, NB, EH, L])
        du = sb("du", [P, NB, EH, L])

        decay = [sb(f"decay{i}", [P, NG, L]) for i in range(N_DECAY)]
        state = [sb(f"state{i}", [P, NG, L]) for i in range(N_STATE)]
        prod = [sb(f"prod{i}", [P, NG, L]) for i in range(N_PROD)]
        c_rep = [sb(f"c_rep{i}", [P, NG, L]) for i in range(N_CREP)]

        ln_stats = sb("ln_stats", [P, NB * KD, 6])
        ln_mv = sb("ln_mv", [P, NB * KD, 2])
        ln_ve = sb("ln_ve", [P, NB * KD])
        ln_half = sb("ln_half", [P, NB * KD])
        ln_rstd = sb("ln_rstd", [P, NB * KD])
        ln_shift = sb("ln_shift", [P, NB * KD])
        minus_half = sb("minus_half", [P, NB * KD])
        z_half, gate = dt_x, dt_ln
        z_tanh = sb("z_tanh", [P, EH, L])

        mixed = sb("mixed", [P, EH, L])
        x1_sb = conv_rep[:].rearrange("p (b t) l -> p b t l", b=2)
        st2 = sb("st2", [P, NB * KD, 6])
        mv2 = sb("mv2", [P, NB * KD, 2])
        ve2 = sb("ve2", [P, NB * KD])
        rstd2 = sb("rstd2", [P, NB * KD])
        shift2 = sb("shift2", [P, NB * KD])
        z2_sb = sb("z2_sb", [P, KD, L])
        z2_hi = sb("z2_hi", [P, KD, L], BF16)
        z2_rest = sb("z2_rest", [P, KD, L])
        z2_mid = sb("z2_mid", [P, KD, L], BF16)
        z2_lo = sb("z2_lo", [P, KD, L], BF16)
        up_tanh = sb("up_tanh", [P, 2, L])
        hidden = sb("hidden", [P, 2, HC, L])

        ps_b = psum("ps_b", 2 * QW)
        ps_db = psum("ps_db", 2 * QW)
        ps_t = psum("ps_t", QW)
        ps_y = psum("ps_y", QW)
        ps_w0 = psum("ps_w0", QW)
        ps_w1 = psum("ps_w1", QW)

        ld_par, ld_win, ld_ctx0, ld_ctx, ld_xw, ld_dtw = (sem(n) for n in (
            "ld_par", "ld_win", "ld_ctx0", "ld_ctx", "ld_xw", "ld_dtw"))
        ld_g, ld_x, ld_w1, ld_w2, ld_w3, ld_w3l = (sem(n) for n in (
            "ld_g", "ld_x", "ld_w1", "ld_w2", "ld_w3", "ld_w3l"))
        ident_ready, rows_ready, const_ready = sem("ident_ready"), sem("rows_ready"), sem("const_ready")
        pool_init = sem("pool_init")
        pick_ready = sem("pick_ready")
        c_loaded = [sem(f"c_loaded{i}") for i in range(N_CREP)]
        half_conv_b_ready, a_exp_ready, a_ready = sem("half_conv_b_ready"), sem("a_exp_ready"), sem("a_ready")
        last_prod_done, last_half_done = sem("last_prod_done"), sem("last_half_done")
        zeros_ready, prod_half_done = sem("zeros_ready"), sem("prod_half_done")
        xw_ready, decay_zeroed = sem("xw_ready"), sem("decay_zeroed")
        tanh_g_ready, half_g_ready = sem("tanh_g_ready"), sem("half_g_ready")
        ld_conv, ld_conv1, ld_conv_b = sem("ld_conv"), sem("ld_conv1"), sem("ld_conv_b")
        ones_row_ready, dt_ones_ready = sem("ones_row_ready"), sem("dt_ones_ready")
        win_tap_ready, conv_done = sem("win_tap_ready"), sem("conv_done")
        conv_tanh_done, u_done = sem("conv_tanh_done"), sem("u_done")
        rows_done, dt_low_done, bc_hi_done = sem("rows_done"), sem("dt_low_done"), sem("bc_hi_done")
        bc_rest_done, bc_mid_done, bc_lo_done = sem("bc_rest_done"), sem("bc_mid_done"), sem("bc_lo_done")
        dt_done, dt_relu_done, dt_abs_done = sem("dt_done"), sem("dt_relu_done"), sem("dt_abs_done")
        dt_exp_done, dt_ln_done = sem("dt_exp_done"), sem("dt_ln_done")
        delta_done, du_done = sem("delta_done"), sem("du_done")
        b_rep_done, bc_rows_done, c_stored = sem("b_rep_done"), sem("bc_rows_done"), sem("c_stored")
        decay_done, db_done, scan_done = sem("decay_done"), sem("db_done"), sem("scan_done")
        prod_done, sum_done = sem("prod_done"), sem("sum_done")
        abs_zeroed, abs_done, gamma_done = sem("abs_zeroed"), sem("abs_done"), sem("gamma_done")
        thr_step, below_done, quant_done = sem("thr_step"), sem("below_done"), sem("quant_done")
        stats_done, mv_done, ve_done = sem("stats_done"), sem("mv_done"), sem("ve_done")
        rstd_done, ln_half_done = sem("rstd_done"), sem("ln_half_done")
        z_half_done, z_tanh_done, gate_done = sem("z_half_done"), sem("z_tanh_done"), sem("gate_done")
        diag_d_ready, mixed_done, mixed_t_done = sem("diag_d_ready"), sem("mixed_done"), sem("mixed_t_done")
        x1_done, st2_done, mv2_done = sem("x1_done"), sem("st2_done"), sem("mv2_done")
        ve2_done, rstd2_done, shift2_done = sem("ve2_done"), sem("rstd2_done"), sem("shift2_done")
        z2_done, z2_t_done, hi_done = sem("z2_done"), sem("z2_t_done"), sem("hi_done")
        rest_done, mid_done, lo_done = sem("rest_done"), sem("mid_done"), sem("lo_done")
        up_done, up_tanh_done, hidden_done = sem("up_done"), sem("up_tanh_done"), sem("hidden_done")
        down_done, out_done, stored = sem("down_done"), sem("out_done"), sem("stored")

        def halves(b):
            return ((0, 1), (1, 1)) if b == 0 else ((0, EH),)

        def conv_bank(b, e):
            return ((ps_w0, ps_db), (ps_y, ps_y), (ps_w0, ps_w0), (ps_w1, ps_w1))[b][e]

        def up_bank(h):
            return ps_t if h % 2 else ps_w0

        block = es.enter_context(nc.Block())

        @block.sync
        def _(sp):
            sp.dma_start(conv_rep[:, :, 0:P], convT[0:DC, 0:P].partition_broadcast(P)).then_inc(ld_conv, 16)
            sp.dma_start(win_sb[:], winT).then_inc(ld_win, 16)
            sp.dma_start(conv_b[:], convT[DC:DC + 1, :]).then_inc(ld_conv_b, 16)
            sp.dma_start(ctx_sb[:, 0, :], ctxT[:, 0, :]).then_inc(ld_ctx0, 16)
            sp.dma_start(conv_rep[:, :, P:DI], convT[0:DC, P:DI].partition_broadcast(P)).then_inc(ld_conv1, 16)
            sp.dma_start(par_sb[:], par.rearrange("(h p) c -> p h c", p=P)).then_inc(ld_par, 16)
            sp.dma_start(xw_in[:], xwT.rearrange("(h p) c -> p h c", p=P)).then_inc(ld_xw, 16)
            sp.dma_start(dtw_sb[DT0:DT0 + DR + 1, :], dtwT).then_inc(ld_dtw, 16)
            sp.dma_start(gains_sb[:], gains.partition_broadcast(P)).then_inc(ld_g, 16)
            sp.dma_start(x_sb[:], x.rearrange("b (t p) d -> p b t d", p=P)).then_inc(ld_x, 16)
            sp.dma_start(ctx_sb[:, 1:NB, :], ctxT[:, 1:NB, :]).then_inc(ld_ctx, 16)
            sp.dma_start(w_up_in[:, 0], w1T.rearrange("(k p) h -> p k h", p=P)).then_inc(ld_w1, 16)
            sp.dma_start(w_up_in[:, 1], w2T.rearrange("(k p) h -> p k h", p=P)).then_inc(ld_w2, 16)
            sp.dma_start(w_down_in[:, 0:HF, :],
                         w3T[0:HF * P, :].rearrange("(c p) d -> p c d", p=P)).then_inc(ld_w3, 16)
            sp.dma_start(w_down_in[0:HL, HF, :], w3T[HF * P:H, :]).then_inc(ld_w3l, 16)

            def load_c(grp):
                b, g = grp // NGRP, grp % NGRP
                if g == 0:
                    sp.wait_ge(c_stored, 16 * (b + 1))
                if grp >= N_CREP:
                    sp.wait_ge(prod_done, EH * (grp - N_CREP + 1))
                sp.dma_start(c_rep[grp % N_CREP][:], c_rows[b, NG * g:NG * (g + 1), :].partition_broadcast(P)
                             ).then_inc(c_loaded[grp % N_CREP], 16)

            def store(b):
                for t in range(KD):
                    sp.wait_ge(out_done, KD * b + t + 1)
                    sp.dma_start(out[b, t * P:(t + 1) * P, :], x_sb[:, b, t, :]).then_inc(stored, 16)

            for grp in range(NB * NGRP):
                load_c(grp)
                if grp == NB * NGRP - 3:
                    store(0)
            for b in range(1, NB):
                store(b)
            sp.wait_ge(stored, 16 * NB * KD)

        @block.gpsimd
        def _(pool):
            nc.gpsimd.memset(ident[:], 0.0).then_inc(pool_init, 1)
            nc.gpsimd.memset(row_of3[:], 0.0).then_inc(pool_init, 1)
            pool.wait_ge(pool_init, 2)
            nc.gpsimd.affine_select(out=row_of3[:], in_=row_of3[:], compare_op=ALU.not_equal, fill=1.0,
                                    base=0, pattern=[[-1, BC]], channel_multiplier=1).then_inc(pool_init, 1)
            for k in range(1, 3):
                pool.wait_ge(pool_init, 2 + k)
                nc.gpsimd.affine_select(out=row_of3[:], in_=row_of3[:], compare_op=ALU.not_equal, fill=1.0,
                                        base=-BC * k, pattern=[[-1, BC]],
                                        channel_multiplier=1).then_inc(rows_ready if k == 2 else pool_init, 1)
            nc.gpsimd.affine_select(out=ident[:], in_=ident[:], compare_op=ALU.not_equal, fill=1.0,
                                    base=0, pattern=[[-1, P]], channel_multiplier=1).then_inc(ident_ready, 1)
            nc.gpsimd.memset(ones[:], 1.0).then_inc(const_ready, 1)
            nc.gpsimd.memset(minus_half[:], -0.5).then_inc(const_ready, 1)
            nc.gpsimd.memset(abs_sum[:, 3:4], 0.0).then_inc(abs_zeroed, 1)

            def product(t):
                states = slice(0, NG if t < NT - 1 else 1)
                pool.wait_ge(scan_done, 2 * (t + 1) if t < NT - 1 else 2 * t + 1)
                pool.wait_ge(c_loaded[(t // EH) % N_CREP], 16 * (t // EH // N_CREP + 1))
                if t >= N_PROD:
                    pool.wait_ge(sum_done, t - N_PROD + 1)
                nc.gpsimd.tensor_tensor(prod[t % N_PROD][:, states], state[t % N_STATE][:, states],
                                        c_rep[(t // EH) % N_CREP][:, states], ALU.mult).then_inc(prod_done, 1)

            def halve(t):
                pool.wait_ge(prod_done, t + 1)
                nc.gpsimd.tensor_tensor(prod[t % N_PROD][:, 0:2, :], prod[t % N_PROD][:, 0:2, :],
                                        prod[t % N_PROD][:, 2:4, :], ALU.add).then_inc(prod_half_done, 1)

            def own_steps(steps):
                for what, b, h in steps:
                    if what == "delta_u" and b > 1:
                        pool.wait_ge(delta_done, EH * (b + 1))
                        pool.wait_ge(du_done, EH * b)
                        nc.gpsimd.tensor_tensor(du[:, b], delta[:, b], u_sb[:, b], ALU.mult).then_inc(du_done, EH)
                    elif what == "softplus_sum" and b > 1:
                        pool.wait_ge(delta_done, EH * b)
                        pool.wait_ge(dt_ln_done, EH * (b + 1))
                        pool.wait_ge(dt_relu_done, EH * (b + 1))
                        nc.gpsimd.tensor_tensor(delta[:, b], dt_x[:, b], dt_ln[:, b],
                                                ALU.add).then_inc(delta_done, EH)
                    elif what == "diag_d":
                        pool.wait_ge(ident_ready, 1)
                        pool.wait_ge(ld_par, 16)
                        for e in range(EH):
                            nc.gpsimd.tensor_tensor(diag_d[:, e, :], ident[:],
                                                    par_sb[:, e, C_D:C_D + 1].to_broadcast([P, P]),
                                                    ALU.mult).then_inc(diag_d_ready, 1)
                    elif what == "rstd":
                        pool.wait_ge(ve_done, 1)
                        pool.wait_ge(const_ready, 2)
                        nc.gpsimd.tensor_tensor(ln_rstd[:], ln_ve[:], minus_half[:],
                                                ALU.pow).then_inc(rstd_done, 1)
                    elif what == "rstd2":
                        c = slice(KD * b, KD * b + KD)
                        pool.wait_ge(ve2_done, b + 1)
                        nc.gpsimd.tensor_tensor(rstd2[:, c], ve2[:, c], minus_half[:, c],
                                                ALU.pow).then_inc(rstd2_done, 1)

            own_steps([("diag_d", 0, 0)])
            for s in range(len(after)):
                own_steps(before[s])
                if s < NT:
                    product(s)
                own_steps(middle[s])
                if s in HALVED:
                    halve(s)
                own_steps(after[s])

        @block.scalar
        def _(act):
            def conv_tanh(b):
                for e, n in halves(b):
                    act.wait_ge(conv_done, EH * b + e + n)
                    nc.scalar.activation(conv_th[:, b, e:e + n],
                                         conv_bank(b, e)[:, e * L:(e + n) * L].rearrange("p (e l) -> p e l", e=n),
                                         ACT.Tanh).then_inc(conv_tanh_done, n)

            def split_rows(b):
                act.wait_ge(rows_done, b + 1)
                act.wait_ge(dt_ones_ready, 1)
                if b >= 2:
                    act.wait_ge(dt_done, b - 1)
                nc.scalar.activation(dt_low[DT0:DT0 + DR, b % 2, :], ps_w1[DT0:DT0 + DR, 0:L],
                                     ACT.Copy).then_inc(dt_low_done, 1)
                if b >= 2:
                    act.wait_ge(c_stored, 16 * (b - 1))
                nc.scalar.activation(bc_rows[:, b % 2, :], ps_w1[0:BC, 0:L], ACT.Copy).then_inc(bc_rows_done, 1)
                nc.scalar.activation(bc_parts[:, b, :], ps_w1[0:3 * BC, 0:L],
                                     ACT.Copy).then_inc(bc_hi_done, 1)
                if b > 0:
                    act.wait_ge(c_stored, 16 * b)
                act.wait_ge(bc_rows_done, b + 1)
                nc.scalar.dma_start(c_rows[b], bc_rows[DS:BC, b % 2, :]).then_inc(c_stored, 16)

            def abs_dt(b):
                act.wait_ge(dt_done, b + 1)
                for e, n in halves(b):
                    nc.scalar.activation(dt_abs[:, b, e:e + n],
                                         ps_w0[:, e * L:(e + n) * L].rearrange("p (e l) -> p e l", e=n),
                                         ACT.Abs).then_inc(dt_abs_done, n)

            def relu_dt(b):
                nc.scalar.activation(dt_x[:, b], ps_w0[:].rearrange("p (e l) -> p e l", e=EH),
                                     ACT.Relu).then_inc(dt_relu_done, EH)

            log_table = [False]

            def softplus_log(b):
                if not log_table[0]:
                    nc.scalar.preload_act_table_set("natural_log_exp_and_others")
                log_table[0] = True
                for e, n in halves(b):
                    act.wait_ge(dt_abs_done, EH * b + e + n)
                    nc.scalar.activation(dt_abs[:, b, e:e + n], dt_abs[:, b, e:e + n], ACT.Exp,
                                         scale=-1.0).then_inc(dt_exp_done, n)
                for e, n in halves(b):
                    act.wait_ge(dt_exp_done, EH * b + e + n)
                    nc.scalar.activation(dt_ln[:, b, e:e + n], dt_abs[:, b, e:e + n], ACT.Ln,
                                         bias=1.0).then_inc(dt_ln_done, n)

            def decays(t):
                b, g, e = t // TPB, (t % TPB) // EH, t % EH
                if t == 0:
                    act.wait_ge(a_ready, 1)
                    act.wait_ge(decay_zeroed, N_DECAY)
                if t == 0 or t % TPB == 0 and b > 0:
                    act.wait_ge(delta_done, EH * b + (1 if b == 0 else EH))
                elif t == 1:
                    act.wait_ge(delta_done, EH)
                if t >= N_DECAY:
                    act.wait_ge(scan_done, 2 * (t - N_DECAY + 1))
                for n in range(NG):
                    last = nc.scalar.activation(decay[t % N_DECAY][:, n, 1:L], delta[:, b, e, 1:L], ACT.Exp,
                                                scale=a_neg[:, e, NG * g + n:NG * g + n + 1])
                    if n % 2 == 1:
                        last.then_inc(decay_done, 1)

            def own_steps(steps):
                for what, b, h in steps:
                    if "tanh" in what:
                        log_table[0] = False
                    if what == "conv_tanh":
                        conv_tanh(b)
                    elif what == "split_rows":
                        split_rows(b)
                    elif what == "abs_dt":
                        abs_dt(b)
                    elif what == "relu_dt":
                        relu_dt(b)
                    elif what == "mid_rows":
                        act.wait_ge(bc_rest_done, b + 1)
                        nc.scalar.activation(bc_mid[2 * BC:3 * BC, b, :], bc_rest[2 * BC:3 * BC, b % 2, :],
                                             ACT.Copy).then_inc(bc_mid_done, 1)
                        nc.scalar.activation(bc_parts[BC:2 * BC, b, :], bc_rest[BC:2 * BC, b % 2, :],
                                             ACT.Copy).then_inc(bc_mid_done, 1)
                    elif what == "softplus_log":
                        softplus_log(b)
                    elif what == "abs_w":
                        if b > 0:
                            act.wait_ge(abs_done, b)
                        if b < 2:
                            act.wait_ge((ld_w1, ld_w2)[b], 16)
                            nc.scalar.activation(w_below[:, 0:KD * H], w_up_in[:, b], ACT.Abs,
                                                 accum_out=abs_sum[:, b:b + 1]).then_inc(abs_done, 1)
                        else:
                            act.wait_ge(ld_w3, 16)
                            nc.scalar.activation(w_below[:, 0:HF * L], w_down_in[:, 0:HF, :], ACT.Abs,
                                                 accum_out=abs_sum[:, 2:3]).then_inc(abs_done, 1)
                            act.wait_ge(ld_w3l, 16)
                            act.wait_ge(abs_zeroed, 1)
                            act.wait_ge(abs_done, 3)
                            nc.scalar.activation(w_below[0:HL, 0:L], w_down_in[0:HL, HF, :], ACT.Abs,
                                                 accum_out=abs_sum[0:HL, 3:4]).then_inc(abs_done, 1)
                    elif what == "z_half":
                        if b == 0:
                            act.wait_ge(ln_half_done, 2)
                        act.wait_ge(delta_done, EH * (b + 1))
                        for e in range(EH):
                            c = KD * b + e
                            nc.scalar.activation(z_half[:, b, e, :], x_sb[:, b, e, :], ACT.Identity,
                                                 bias=ln_shift[:, c:c + 1],
                                                 scale=ln_half[:, c:c + 1]).then_inc(z_half_done, 1)
                    elif what == "z_tanh":
                        act.wait_ge(z_half_done, EH * (b + 1))
                        if b > 0:
                            act.wait_ge(gate_done, b)
                        nc.scalar.activation(z_tanh[:], z_half[:, b], ACT.Tanh).then_inc(z_tanh_done, 1)
                    elif what == "z2_hi":
                        act.wait_ge(z2_t_done, b + 1)
                        if b > 0:
                            act.wait_ge(up_done, HC * b)
                        nc.scalar.activation(z2_hi[:], ps_t[:].rearrange("p (k l) -> p k l", k=KD),
                                             ACT.Copy).then_inc(hi_done, 1)
                    elif what == "z2_mid":
                        act.wait_ge(rest_done, b + 1)
                        nc.scalar.activation(z2_mid[:], z2_rest[:], ACT.Copy).then_inc(mid_done, 1)
                    elif what == "up_tanh":
                        k = HC * b + h
                        rows = P if h < HF else HL
                        act.wait_ge(up_done, k + 1)
                        if k >= 2:
                            act.wait_ge(hidden_done, k - 1)
                        nc.scalar.activation(up_tanh[0:rows, k % 2, :], up_bank(h)[0:rows, 0:L], ACT.Tanh,
                                             scale=0.5).then_inc(up_tanh_done, 1)

            act.wait_ge(rows_ready, 1)
            nc.scalar.activation(pick[:, 0:DS], row_of3[:, 0:DS, None].to_broadcast([3 * BC, DS, P]),
                                 ACT.Copy).then_inc(pick_ready, 1)
            act.wait_ge(ld_par, 16)
            nc.scalar.activation(a_exp[:], par_sb[:, :, C_ALOG:C_ALOG + DS], ACT.Exp).then_inc(a_exp_ready, 1)
            conv_tanh(0)
            act.wait_ge(ld_g, 16)
            nc.scalar.activation(tanh_g[:], gains_sb[:], ACT.Tanh).then_inc(tanh_g_ready, 1)
            nc.scalar.preload_act_table_set("natural_log_exp_and_others")
            log_table[0] = True
            split_rows(0)
            abs_dt(0)
            softplus_log(0)
            decays(0)
            for s in range(len(after)):
                own_steps(before[s])
                if s + 1 < NT:
                    decays(s + 1)
                own_steps(middle[s])
                own_steps(after[s])

        @block.vector
        def _(dve):
            def silu_conv(b):
                for e, n in halves(b):
                    dve.wait_ge(conv_tanh_done, EH * b + e + n)
                    nc.vector.scalar_tensor_tensor(
                        out=u_sb[:, b, e:e + n], in0=conv_th[:, b, e:e + n], scalar=1.0,
                        in1=conv_bank(b, e)[:, e * L:(e + n) * L].rearrange("p (e l) -> p e l", e=n),
                        op0=ALU.add, op1=ALU.mult).then_inc(u_done, n)

            def rest_rows(b):
                dve.wait_ge(bc_hi_done, b + 1)
                nc.vector.tensor_tensor(bc_rest[:, b % 2, :], ps_w1[0:3 * BC, 0:L], bc_parts[:, b, :],
                                        ALU.subtract).then_inc(bc_rest_done, 1)

            def low_rows(b):
                dve.wait_ge(bc_mid_done, 2 * b + 1)
                low = slice(2 * BC, 3 * BC)
                nc.vector.tensor_tensor(bc_parts[low, b, :], bc_rest[low, b % 2, :], bc_mid[low, b, :],
                                        ALU.subtract).then_inc(bc_lo_done, 1)

            def relu_dt():
                dve.wait_ge(dt_abs_done, EH)
                for e in range(EH):
                    nc.vector.tensor_scalar(dt_x[:, 0, e, :], ps_w0[:, e * L:(e + 1) * L],
                                            0.0, None, ALU.max).then_inc(dt_relu_done, 1)

            def first_delta(e):
                dve.wait_ge(dt_ln_done, e + 1)
                dve.wait_ge(dt_relu_done, e + 1)
                nc.vector.tensor_tensor(delta[:, 0, e], dt_x[:, 0, e], dt_ln[:, 0, e],
                                        ALU.add).then_inc(delta_done, 1)
                dve.wait_ge(delta_done, e + 1)
                nc.vector.tensor_tensor(du[:, 0, e], delta[:, 0, e], u_sb[:, 0, e], ALU.mult).then_inc(du_done, 1)

            def scan_tile(t, between):
                b, g, e = t // TPB, (t % TPB) // EH, t % EH
                grp = t // EH
                if t % TPB == 0:
                    dve.wait_ge(du_done, EH * b + (1 if b == 0 else EH))
                elif t == 1:
                    dve.wait_ge(du_done, EH)
                if e == 0:
                    dve.wait_ge(b_rep_done, grp + 1)
                for q in range(2):
                    if t >= 1:
                        dve.wait_ge(scan_done, 2 * (t - 1) + q + 1)
                    nc.vector.tensor_tensor(
                        ps_db[:, q * QW:(q + 1) * QW].rearrange("p (n l) -> p n l", n=2),
                        du[:, b, e, None, :].to_broadcast([P, 2, L]),
                        ps_b[:, q * QW:(q + 1) * QW].rearrange("p (n l) -> p n l", n=2),
                        ALU.mult).then_inc(db_done, 1)
                own_steps(between)
                if t == 0:
                    first_delta(1)
                if t >= N_STATE:
                    dve.wait_ge(prod_done, t - N_STATE + 1)
                for q in range(2):
                    dve.wait_ge(decay_done, 2 * t + q + 1)
                    dve.wait_ge(db_done, 2 * t + q + 1)
                    nc.vector.tensor_tensor_scan(
                        state[t % N_STATE][:].rearrange("p n l -> p (n l)")[:, q * QW:(q + 1) * QW],
                        decay[t % N_DECAY][:].rearrange("p n l -> p (n l)")[:, q * QW:(q + 1) * QW],
                        ps_db[:, q * QW:(q + 1) * QW], 0.0, ALU.mult, ALU.add).then_inc(scan_done, 1)

            def last_product():
                t = NT - 1
                dve.wait_ge(scan_done, 2 * NT)
                dve.wait_ge(c_loaded[(t // EH) % N_CREP], 16 * (t // EH // N_CREP + 1))
                dve.wait_ge(sum_done, t - N_PROD + 1)
                nc.vector.tensor_tensor(prod[t % N_PROD][:, 1:NG], state[t % N_STATE][:, 1:NG],
                                        c_rep[(t // EH) % N_CREP][:, 1:NG], ALU.mult).then_inc(last_prod_done, 1)
                dve.wait_ge(last_prod_done, 1)
                dve.wait_ge(prod_done, NT)
                nc.vector.tensor_tensor(prod[t % N_PROD][:, 0:2, :], prod[t % N_PROD][:, 0:2, :],
                                        prod[t % N_PROD][:, 2:4, :], ALU.add).then_inc(last_half_done, 1)

            nc.vector.memset(zeros[:], 0.0).then_inc(zeros_ready, 1)
            nc.vector.memset(ones_row[:], 1.0).then_inc(ones_row_ready, 1)
            nc.vector.memset(dt_low[DT0:DT0 + DR + 1], 1.0).then_inc(dt_ones_ready, 1)
            dve.wait_ge(ld_win, 16)
            for e in range(EH):
                dve.wait_ge((ld_conv, ld_conv1)[e], 16)
                if e == 1:
                    dve.wait_ge(ld_conv_b, 16)
                    nc.vector.tensor_scalar(half_conv_b[:], conv_b[:], 0.5, None,
                                            ALU.mult).then_inc(half_conv_b_ready, 1)
                cs = slice(e * P, (e + 1) * P)
                nc.vector.scalar_tensor_tensor(
                    out=win_tap[:, :, cs], in0=conv_rep[:, :, cs], scalar=0.5,
                    in1=win_sb[:, None, cs].to_broadcast([P, DC, P]), op0=ALU.mult,
                    op1=ALU.mult).then_inc(win_tap_ready, 1)
            dve.wait_ge(ld_xw, 16)
            for k in range(3):
                nc.vector.tensor_copy(xw_sb[:, :, k * BC:(k + 1) * BC], xw_in[:, :, 0:BC]).then_inc(xw_ready, 1)
            nc.vector.tensor_copy(xw_sb[:, :, DT0:DT0 + DR], xw_in[:, :, BC:BC + DR]).then_inc(xw_ready, 1)
            for i in range(N_DECAY):
                nc.vector.memset(decay[i][:, :, 0:1], 0.0).then_inc(decay_zeroed, 1)
            def own_steps(steps):
                for what, b, h in steps:
                    if what == "silu_conv":
                        silu_conv(b)
                    elif what == "rest_rows":
                        if b >= 2:
                            dve.wait_ge(bc_lo_done, b - 1)
                            dve.wait_ge(bc_mid_done, 2 * (b - 1))
                        rest_rows(b)
                    elif what == "low_rows":
                        low_rows(b)
                    elif what == "stats":
                        dve.wait_ge(ld_x, 16)
                        cs = range(b * NB * KD // 2, (b + 1) * NB * KD // 2)
                        for c in cs:
                            nc.vector.bn_stats(ln_stats[:, c, :], x_sb[:, c // KD, c % KD, :]).then_inc(stats_done, 1)
                        for c in cs:
                            dve.wait_ge(stats_done, c + 1)
                            nc.vector.bn_aggr(ln_mv[:, c, :], ln_stats[:, c, :]).then_inc(mv_done, 1)
                        if b == 1:
                            dve.wait_ge(mv_done, NB * KD)
                            nc.vector.tensor_scalar(ln_ve[:], ln_mv[:, :, 1], LN_EPS, None,
                                                    ALU.add).then_inc(ve_done, 1)
                    elif what == "ln_shift":
                        dve.wait_ge(rstd_done, 1)
                        nc.vector.tensor_scalar(ln_half[:], ln_rstd[:], 0.5, None,
                                                ALU.mult).then_inc(ln_half_done, 1)
                        dve.wait_ge(ln_half_done, 1)
                        nc.vector.scalar_tensor_tensor(out=ln_shift[:], in0=ln_mv[:, :, 0], scalar=-1.0,
                                                       in1=ln_half[:], op0=ALU.mult,
                                                       op1=ALU.mult).then_inc(ln_half_done, 1)
                    elif what == "thresholds":
                        dve.wait_ge(gamma_done, 1)
                        nc.vector.tensor_scalar(thr[:, 0:2], ps_w1[:, 0:2], 0.5 / (H * L), 0.5 * Q_EPS,
                                                ALU.mult, ALU.add).then_inc(thr_step, 1)
                        nc.vector.tensor_reduce(thr[:, 3:4], ps_w1[:, 2:4], AX_X, ALU.add).then_inc(thr_step, 1)
                        dve.wait_ge(thr_step, 2)
                        nc.vector.tensor_scalar(thr[:, 2:3], thr[:, 3:4], 0.5 / (H * L), 0.5 * Q_EPS,
                                                ALU.mult, ALU.add).then_inc(thr_step, 1)
                        dve.wait_ge(thr_step, 3)
                        nc.vector.tensor_scalar(thr_neg[:, 0:3], thr[:, 0:3], -1.0, None,
                                                ALU.mult).then_inc(thr_step, 1)
                    elif what == "quant" and b < 2:
                        dve.wait_ge(thr_step, 4)
                        if b > 0:
                            dve.wait_ge(quant_done, 2 * b)
                        below = w_below[:, 0:KD * H].rearrange("p (k h) -> p k h", k=KD)
                        nc.vector.tensor_scalar(below, w_up_in[:, b], thr_neg[:, b:b + 1], None,
                                                ALU.is_lt).then_inc(below_done, 1)
                        dve.wait_ge(below_done, b + 1)
                        full, rest = HF * P, 2 * HF * P + b * HL
                        for src, dst in ((slice(0, full), slice(b * full, (b + 1) * full)),
                                         (slice(full, H), slice(rest, rest + HL))):
                            nc.vector.scalar_tensor_tensor(
                                out=w_up_q[:, :, dst], in0=w_up_in[:, b, :, src], scalar=thr[:, b:b + 1],
                                in1=below[:, :, src], op0=ALU.is_gt, op1=ALU.subtract).then_inc(quant_done, 1)
                    elif what == "quant":
                        dve.wait_ge(quant_done, 4)
                        below = w_below[:, 0:HC * L].rearrange("p (c d) -> p c d", c=HC)
                        for rows, cs in ((P, slice(0, HF)), (HL, slice(HF, HC))):
                            nc.vector.tensor_scalar(below[0:rows, cs], w_down_in[0:rows, cs], thr_neg[0:rows, 2:3],
                                                    None, ALU.is_lt).then_inc(below_done, 1)
                        dve.wait_ge(below_done, 4)
                        for rows, cs in ((P, slice(0, HF)), (HL, slice(HF, HC))):
                            nc.vector.scalar_tensor_tensor(
                                out=w_down_q[0:rows, cs], in0=w_down_in[0:rows, cs], scalar=thr[0:rows, 2:3],
                                in1=below[0:rows, cs], op0=ALU.is_gt, op1=ALU.subtract).then_inc(quant_done, 1)
                    elif what == "softplus_sum" and b == 1:
                        dve.wait_ge(dt_ln_done, EH * 2)
                        dve.wait_ge(dt_relu_done, EH * 2)
                        nc.vector.tensor_tensor(delta[:, 1], dt_x[:, 1], dt_ln[:, 1], ALU.add).then_inc(delta_done, EH)
                    elif what == "delta_u" and b == 1:
                        dve.wait_ge(delta_done, EH * 2)
                        nc.vector.tensor_tensor(du[:, 1], delta[:, 1], u_sb[:, 1], ALU.mult).then_inc(du_done, EH)
                    elif what == "half_gain":
                        dve.wait_ge(tanh_g_ready, 1)
                        nc.vector.tensor_scalar(half_tanh_g[:], tanh_g[:], 0.5, None,
                                                ALU.mult).then_inc(half_g_ready, 1)
                    elif what == "gate":
                        dve.wait_ge(z_tanh_done, b + 1)
                        dve.wait_ge(delta_done, EH * (b + 1))
                        nc.vector.scalar_tensor_tensor(out=gate[:, b], in0=z_tanh[:], scalar=1.0, in1=z_half[:, b],
                                                       op0=ALU.add, op1=ALU.mult).then_inc(gate_done, 1)
                    elif what == "mix":
                        dve.wait_ge(sum_done, TPB * (b + 1))
                        dve.wait_ge(gate_done, b + 1)
                        if b > 0:
                            dve.wait_ge(mixed_t_done, b)
                        nc.vector.scalar_tensor_tensor(
                            out=mixed[:], in0=ps_y[:].rearrange("p (e l) -> p e l", e=EH),
                            scalar=tanh_g[:, 0:1], in1=gate[:, b], op0=ALU.mult, op1=ALU.mult).then_inc(mixed_done, 1)
                    elif what == "x1":
                        dve.wait_ge(mixed_t_done, b + 1)
                        if b >= 2:
                            dve.wait_ge(out_done, KD * (b - 1))
                        nc.vector.tensor_tensor(x1_sb[:, b % 2], x_sb[:, b],
                                                ps_t[:].rearrange("p (t l) -> p t l", t=KD),
                                                ALU.add).then_inc(x1_done, 1)
                        dve.wait_ge(x1_done, b + 1)
                        for t in range(KD):
                            nc.vector.bn_stats(st2[:, KD * b + t, :], x1_sb[:, b % 2, t, :]).then_inc(st2_done, 1)
                        for t in range(KD):
                            dve.wait_ge(st2_done, KD * b + t + 1)
                            nc.vector.bn_aggr(mv2[:, KD * b + t, :], st2[:, KD * b + t, :]).then_inc(mv2_done, 1)
                        dve.wait_ge(mv2_done, KD * (b + 1))
                        c = slice(KD * b, KD * b + KD)
                        nc.vector.tensor_scalar(ve2[:, c], mv2[:, c, 1], LN_EPS, None, ALU.add).then_inc(ve2_done, 1)
                    elif what == "z2_lo":
                        dve.wait_ge(mid_done, b + 1)
                        if b > 0:
                            dve.wait_ge(up_done, HC * b)
                        nc.vector.tensor_tensor(z2_lo[:], z2_rest[:], z2_mid[:],
                                                ALU.subtract).then_inc(lo_done, 1)
                    elif what == "shift2":
                        c = slice(KD * b, KD * b + KD)
                        dve.wait_ge(rstd2_done, b + 1)
                        nc.vector.scalar_tensor_tensor(out=shift2[:, c], in0=mv2[:, c, 0], scalar=-1.0,
                                                       in1=rstd2[:, c], op0=ALU.mult,
                                                       op1=ALU.mult).then_inc(shift2_done, 1)
                    elif what == "z2":
                        dve.wait_ge(shift2_done, b + 1)
                        if b > 0:
                            dve.wait_ge(z2_t_done, b)
                        for t in range(KD):
                            c = KD * b + t
                            nc.vector.tensor_scalar(z2_sb[:, t, :], x1_sb[:, b % 2, t, :], rstd2[:, c:c + 1],
                                                    shift2[:, c:c + 1], ALU.mult, ALU.add).then_inc(z2_done, 1)
                    elif what == "z2_rest":
                        dve.wait_ge(hi_done, b + 1)
                        nc.vector.tensor_tensor(z2_rest[:], ps_t[:].rearrange("p (k l) -> p k l", k=KD),
                                                z2_hi[:], ALU.subtract).then_inc(rest_done, 1)
                    elif what == "hidden":
                        k = HC * b + h
                        rows = P if h < HF else HL
                        dve.wait_ge(up_tanh_done, k + 1)
                        if b >= 2 and h == 0:
                            dve.wait_ge(down_done, b - 1)
                        x2 = up_bank(h)[:, L:2 * L] if h < HF else up_bank(h)[HL:2 * HL, 0:L]
                        nc.vector.scalar_tensor_tensor(out=hidden[0:rows, b % 2, h, :],
                                                       in0=up_tanh[0:rows, k % 2, :], scalar=1.0, in1=x2,
                                                       op0=ALU.add, op1=ALU.mult).then_inc(hidden_done, 1)
                    elif what == "out":
                        dve.wait_ge(down_done, b + 1)
                        for t in range(KD):
                            nc.vector.scalar_tensor_tensor(
                                out=x_sb[:, b, t, :], in0=ps_w1[:, t * L:(t + 1) * L],
                                scalar=half_tanh_g[:, 1:2], in1=x1_sb[:, b % 2, t, :],
                                op0=ALU.mult, op1=ALU.add).then_inc(out_done, 1)

            dve.wait_ge(a_exp_ready, 1)
            nc.vector.tensor_scalar(a_neg[:], a_exp[:], -1.0, None, ALU.mult).then_inc(a_ready, 1)
            silu_conv(0)
            own_steps([("stats", 0, 0)])
            rest_rows(0)
            dve.wait_ge(bc_rest_done, 1)
            nc.vector.tensor_copy(bc_mid[2 * BC:3 * BC, 0, :], bc_rest[2 * BC:3 * BC, 0, :]).then_inc(bc_mid_done, 1)
            nc.vector.tensor_copy(bc_parts[BC:2 * BC, 0, :], bc_rest[BC:2 * BC, 0, :]).then_inc(bc_mid_done, 1)
            low_rows(0)
            relu_dt()
            first_delta(0)
            for s in range(len(after)):
                if s == 1:
                    own_steps([("half_gain", 0, 0)])
                own_steps(before[s])
                if s < NT:
                    scan_tile(s, middle[s])
                    if s == NT - 1:
                        last_product()
                else:
                    own_steps(middle[s])
                own_steps(after[s])

        @block.tensor
        def _(pe):
            issued = {step: 0 for step in ("conv", "rows", "dt", "gamma", "mix_t", "z2_t", "up")}

            def convolve(b):
                if b < 2:
                    pe.wait_ge(ld_ctx0 if b == 0 else ld_ctx, 16)
                if b == 2:
                    pe.wait_ge(dt_relu_done, EH * issued["dt"])
                elif b == 3:
                    pe.wait_ge(bc_rest_done, issued["rows"])
                    if issued["gamma"] > 0:
                        pe.wait_ge(thr_step, 2)
                issued["conv"] += 1
                for e in range(EH):
                    if b == 0:
                        pe.wait_ge(win_tap_ready, e + 1)
                    for k in range(DC):
                        nc.tensor.matmul(conv_bank(b, e)[:, e * L + k:(e + 1) * L],
                                         win_tap[:, DC - 1 - k, e * P:(e + 1) * P],
                                         ctx_sb[:, b, 0:L - k], start=(k == 0), stop=False,
                                         skip_group_check=True)
                    if b == 0:
                        pe.wait_ge(half_conv_b_ready, 1)
                        pe.wait_ge(ones_row_ready, 1)
                    last = nc.tensor.matmul(conv_bank(b, e)[:, e * L:(e + 1) * L],
                                            half_conv_b[:, e * P:(e + 1) * P], ones_row[:], start=False,
                                            stop=True, skip_group_check=True)
                    last.then_inc(conv_done, 1)

            def rows_bc_dt(b):
                if b == 0:
                    pe.wait_ge(xw_ready, 4)
                if b > 0:
                    pe.wait_ge(bc_rest_done, b)
                if issued["gamma"] > 0:
                    pe.wait_ge(thr_step, 2)
                if issued["conv"] == NB:
                    pe.wait_ge(u_done, EH * NB)
                issued["rows"] += 1
                for e in range(EH):
                    pe.wait_ge(u_done, EH * b + (e if b == 0 else EH - 1) + 1)
                    last = nc.tensor.matmul(ps_w1[0:DT0 + DR, 0:L], xw_sb[:, e, :], u_sb[:, b, e, :],
                                            start=(e == 0), stop=(e == EH - 1))
                last.then_inc(rows_done, 1)

            def project_dt(b):
                if b == 0:
                    pe.wait_ge(ld_dtw, 16)
                if b > 0:
                    pe.wait_ge(dt_relu_done, EH * b)
                if issued["conv"] >= 3:
                    pe.wait_ge(u_done, EH * 3)
                issued["dt"] += 1
                pe.wait_ge(dt_low_done, b + 1)
                for e in range(EH):
                    last = nc.tensor.matmul(ps_w0[:, e * L:(e + 1) * L],
                                            dtw_sb[DT0:DT0 + DR + 1, e * P:(e + 1) * P],
                                            dt_low[DT0:DT0 + DR + 1, b % 2, :], start=True, stop=True)
                last.then_inc(dt_done, 1)

            def spread_b(grp):
                b, g = grp // NGRP, grp % NGRP
                if g == 0:
                    pe.wait_ge(bc_mid_done, 2 * (b + 1))
                    pe.wait_ge(bc_lo_done, b + 1)
                if grp == 0:
                    pe.wait_ge(pick_ready, 1)
                else:
                    pe.wait_ge(db_done, 2 * EH * grp)
                for n in range(NG):
                    last = nc.tensor.matmul(ps_b[:, n * L:(n + 1) * L], pick[:, NG * g + n, :],
                                            bc_parts[:, b, :], start=True, stop=True)
                last.then_inc(b_rep_done, 1)

            def sum_states(t):
                b, g, e = t // TPB, (t % TPB) // EH, t % EH
                if t == NT - 1:
                    pe.wait_ge(last_half_done, 1)
                elif t in HALVED:
                    pe.wait_ge(prod_half_done, HALVED.index(t) + 1)
                else:
                    pe.wait_ge(prod_done, t + 1)
                left = NG // 2 if t in HALVED or t == NT - 1 else NG
                if t % TPB == 0:
                    if b == 0:
                        pe.wait_ge(u_done, EH * 2)
                    else:
                        pe.wait_ge(mixed_done, b)
                    if b == 0:
                        pe.wait_ge(diag_d_ready, EH)
                    for half in range(EH):
                        nc.tensor.matmul(ps_y[:, half * L:(half + 1) * L], diag_d[:, half, :], u_sb[:, b, half, :],
                                         start=(half == 0), stop=False, skip_group_check=True)
                for n in range(left):
                    last = nc.tensor.matmul(ps_y[:, e * L:(e + 1) * L], ident[:], prod[t % N_PROD][:, n, :],
                                            start=False,
                                            stop=(t % TPB == TPB - 1 and n == left - 1), skip_group_check=True)
                last.then_inc(sum_done, 1)

            def own_steps(steps):
                for what, b, h in steps:
                    if what == "conv":
                        convolve(b)
                    elif what == "rows":
                        rows_bc_dt(b)
                    elif what == "dt":
                        project_dt(b)
                    elif what == "gamma":
                        pe.wait_ge(abs_done, 4)
                        pe.wait_ge(const_ready, 2)
                        pe.wait_ge(bc_rest_done, issued["rows"])
                        if issued["conv"] == NB:
                            pe.wait_ge(u_done, EH * NB)
                        issued["gamma"] += 1
                        nc.tensor.matmul(ps_w1[:, 0:4], ones[:], abs_sum[:], start=True,
                                         stop=True).then_inc(gamma_done, 1)
                    elif what == "mix_t":
                        pe.wait_ge(mixed_done, b + 1)
                        if b > 0:
                            pe.wait_ge(rest_done, b)
                        if issued["up"] > 1:
                            pe.wait_ge(hidden_done, issued["up"] // 2 * 2)
                        issued["mix_t"] += 1
                        for t in range(KD):
                            for e in range(EH):
                                last = nc.tensor.transpose(ps_t[:, t * L + e * P:t * L + (e + 1) * P],
                                                           mixed[:, e, t * P:(t + 1) * P], ident[:])
                        last.then_inc(mixed_t_done, 1)
                    elif what == "z2_t":
                        pe.wait_ge(z2_done, KD * (b + 1))
                        pe.wait_ge(x1_done, b + 1)
                        if issued["up"] > 1:
                            pe.wait_ge(hidden_done, issued["up"] // 2 * 2)
                        issued["z2_t"] += 1
                        for k in range(KD):
                            for t in range(KD):
                                last = nc.tensor.transpose(ps_t[:, k * L + t * P:k * L + (t + 1) * P],
                                                           z2_sb[:, t, k * P:(k + 1) * P], ident[:])
                        last.then_inc(z2_t_done, 1)
                    elif what == "up":
                        k = HC * b + h
                        if h == 0 and b == 0:
                            pe.wait_ge(quant_done, 4)
                        if k == 0:
                            pe.wait_ge(dt_relu_done, EH * NB)
                        elif h % 2:
                            pe.wait_ge(x1_done, issued["mix_t"])
                            pe.wait_ge(rest_done, issued["z2_t"])
                        if k >= 2:
                            pe.wait_ge(hidden_done, k - 1)
                        issued["up"] += 1
                        bank = up_bank(h)
                        if h < HF:
                            cols = ((h * P, slice(0, L)), ((HF + h) * P, slice(L, 2 * L)))
                        else:
                            cols = ((2 * HF * P, slice(0, L)),)
                        for i, (z, split_done) in enumerate(((z2_hi, hi_done), (z2_mid, mid_done), (z2_lo, lo_done))):
                            if h == 0:
                                pe.wait_ge(split_done, b + 1)
                            for j, (at, where) in enumerate(cols):
                                for kd in range(KD):
                                    last = nc.tensor.matmul(bank[:, where], w_up_q[:, kd, at:at + P], z[:, kd, :],
                                                            start=(i == 0 and j == 0 and kd == 0),
                                                            stop=(i == 2 and j == len(cols) - 1 and kd == KD - 1),
                                                            skip_group_check=True)
                        last.then_inc(up_done, 1)
                    elif what == "down":
                        rows = P if h < HF else HL
                        pe.wait_ge(hidden_done, HC * b + h + 1)
                        if h == 0:
                            if b == 0:
                                pe.wait_ge(quant_done, 6)
                                pe.wait_ge(bc_rest_done, NB)
                                pe.wait_ge(thr_step, 2)
                            else:
                                pe.wait_ge(out_done, KD * b)
                        for t in range(KD):
                            last = nc.tensor.matmul(ps_w1[:, t * L:(t + 1) * L],
                                                    hidden[0:rows, b % 2, h, t * P:(t + 1) * P],
                                                    w_down_q[0:rows, h, :], start=(h == 0 and t == 0),
                                                    stop=(h == HC - 1 and t == KD - 1), skip_group_check=True)
                        if h == HC - 1:
                            last.then_inc(down_done, 1)

            pe.wait_ge(zeros_ready, 1)
            for i in range(N_WARM):
                nc.tensor.matmul(ps_w1[:], zeros[:, 0:P], zeros[:], start=True, stop=True)
            convolve(0)
            rows_bc_dt(0)
            project_dt(0)
            spread_b(0)
            for s in range(len(after)):
                own_steps(before[s])
                if s == 0:
                    pe.wait_ge(ident_ready, 1)
                if LAG <= s < NT:
                    sum_states(s - LAG)
                if s == NT:
                    for t in range(NT - LAG, NT - 1):
                        sum_states(t)
                own_steps(middle[s])
                if s == NT:
                    sum_states(NT - 1)
                if s % 2 == 1 and s + 1 < NT:
                    spread_b((s + 1) // 2)
                own_steps(after[s])


def kernel(**inputs):
    import numpy as np
    import concourse.bacc as bacc
    from concourse.bass_utils import run_bass_kernel_spmd

    a = {k: np.asarray(v) for k, v in inputs.items()}
    pre = "L0_xattn_"
    xw = a[pre + "x_proj_w"]
    arrays = {
        "x": a["x"],
        "ctxT": a["ctx_1024"].transpose(2, 0, 1),
        "gains": np.concatenate([a["g_xattn"], a["g_ffn"]]),
        "winT": a[pre + "in_proj_w"].T,
        "convT": np.concatenate([a[pre + "conv_w"].T, a[pre + "conv_b"][None]]),
        "par": np.concatenate([a[pre + "A_log"], a[pre + "D"][:, None]], axis=1),
        "xwT": np.concatenate([xw[DR:], xw[:DR]], axis=0).T,
        "dtwT": np.concatenate([a[pre + "dt_proj_w"].T, a[pre + "dt_proj_b"][None]]),
        "w1T": a["L0_ffn_w1"].T,
        "w2T": a["L0_ffn_w2"].T,
        "w3T": a["L0_ffn_w3"].T,
    }
    nc = bacc.Bacc("TRN2", target_bir_lowering=False, num_devices=1)
    ins, args = {}, []
    for name, v in arrays.items():
        v = np.ascontiguousarray(v)
        ins[f"in_{name}"] = v
        args.append(nc.dram_tensor(f"in_{name}", v.shape, mybir.dt.from_np(v.dtype), kind="ExternalInput").ap())
    c_rows = nc.dram_tensor("c_rows", (NB, DS, L), F32, kind="Internal").ap()
    out = nc.dram_tensor("out_0", (NB, L, L), F32, kind="ExternalOutput").ap()
    gated_ssm_ffn_kernel(nc, *args, c_rows, out)
    r = run_bass_kernel_spmd(nc, [ins], core_ids=[0])
    return r.results[0]["out_0"]
```
